# Optimizing a Trainium2 kernel written in Bass

```python
import numpy as np
import jax
import jax.numpy as jnp

def _softmax(x, axis=-1):
    return jax.nn.softmax(x, axis=axis)

def _gelu(x):
    return jax.nn.gelu(x, approximate=True)

def _silu(x):
    return jax.nn.silu(x)

def _sigmoid(x):
    return jax.nn.sigmoid(x)

def _layernorm(x, axis=-1, eps=1e-05):
    m = jnp.mean(x, axis=axis, keepdims=True)
    v = jnp.var(x, axis=axis, keepdims=True)
    return (x - m) / jnp.sqrt(v + eps)

def _scatter_add(tgt, idx, src, axis=0):
    return tgt.at[idx].add(src)

def _segment_sum(src, seg, n):
    return jax.ops.segment_sum(src, seg, n)
kernel_name = 'mk_recurrent_d1_jaxref_r8_1c3831'

def setup_inputs(seed: int=0):
    np.random.seed(seed)
    _w = jnp.asarray

    def _L0_attn_setup():
        import jax, jax.numpy as jnp
        import numpy as np
        B, S, E, H, ML = (4, 128, 128, 16, 256)
        HD = E // H

        def _layernorm(x, g, b, eps=1e-05):
            m = x.mean(-1, keepdims=True)
            v = ((x - m) ** 2).mean(-1, keepdims=True)
            return (x - m) * jax.lax.rsqrt(v + eps) * g + b

        def _causal_mask(size, rel_pos):
            flipped = jnp.flip(rel_pos[:, :size], -1)
            neg_inf = jnp.full((rel_pos.shape[0], size), -jnp.inf, rel_pos.dtype)
            padded = jnp.concatenate([flipped, neg_inf], axis=-1)
            idx = jnp.arange(size)[None, :] - jnp.arange(size)[:, None] + size - 1
            return padded[:, idx]
        key = jax.random.key(seed)
        ks = jax.random.split(key, 8)
        s = 0.02
        return {'x': jax.random.normal(ks[0], (B, S, E), dtype=jnp.float32), 'rel_pos': jax.random.normal(ks[1], (H, ML), dtype=jnp.float32), 'in_proj_w': jax.random.normal(ks[2], (3 * E, E), dtype=jnp.float32) * s, 'in_proj_b': jnp.zeros((3 * E,), jnp.float32), 'out_w': jax.random.normal(ks[3], (E, E), dtype=jnp.float32) * s, 'out_b': jnp.zeros((E,), jnp.float32), 'w1': jax.random.normal(ks[4], (4 * E, E), dtype=jnp.float32) * s, 'b1': jnp.zeros((4 * E,), jnp.float32), 'w2': jax.random.normal(ks[5], (E, 4 * E), dtype=jnp.float32) * s, 'b2': jnp.zeros((E,), jnp.float32), 'ln1_g': jnp.ones((E,), jnp.float32), 'ln1_b': jnp.zeros((E,), jnp.float32), 'ln2_g': jnp.ones((E,), jnp.float32), 'ln2_b': jnp.zeros((E,), jnp.float32)}
    _L0_attn_in = _L0_attn_setup()

    def _L0_ffn_setup():
        import jax, jax.numpy as jnp
        import numpy as np
        DIM = 128

        def _reference_tuple_inner(x, W_r, W_k, W_v, mu_r, mu_k):
            B, T, C = x.shape
            x_prev = jnp.concatenate([jnp.zeros((B, 1, C), x.dtype), x[:, :-1, :]], axis=1)
            xr = mu_r * x + (1.0 - mu_r) * x_prev
            xk = mu_k * x + (1.0 - mu_k) * x_prev
            r = jax.nn.sigmoid(jnp.einsum('btc,dc->btd', xr, W_r))
            k = jnp.einsum('btc,dc->btd', xk, W_k)
            k_act = jnp.square(jax.nn.relu(k))
            out = r * jnp.einsum('btc,dc->btd', k_act, W_v)
            new_state = x[:, -1, :]
            return (out, new_state)
        key = jax.random.key(seed)
        ks = jax.random.split(key, 6)
        B, T, C = (8, 256, DIM)
        x = jax.random.normal(ks[0], (B, T, C), dtype=jnp.float32)
        s = 1.0 / np.sqrt(C)
        W_r = jax.random.uniform(ks[1], (C, C), jnp.float32, -s, s)
        W_k = jax.random.uniform(ks[2], (C, C), jnp.float32, -s, s)
        W_v = jax.random.uniform(ks[3], (C, C), jnp.float32, -s, s)
        mu_r = jax.random.uniform(ks[4], (C,), jnp.float32)
        mu_k = jax.random.uniform(ks[5], (C,), jnp.float32)
        return {'x': x, 'W_r': W_r, 'W_k': W_k, 'W_v': W_v, 'mu_r': mu_r, 'mu_k': mu_k}
    _L0_ffn_in = _L0_ffn_setup()
    _d = {'L0_attn_x': _L0_attn_in['x'], 'L0_attn_rel_pos': _L0_attn_in['rel_pos'], 'L0_attn_in_proj_w': _L0_attn_in['in_proj_w'], 'L0_attn_in_proj_b': _L0_attn_in['in_proj_b'], 'L0_attn_out_w': _L0_attn_in['out_w'], 'L0_attn_out_b': _L0_attn_in['out_b'], 'L0_attn_w1': _L0_attn_in['w1'], 'L0_attn_b1': _L0_attn_in['b1'], 'L0_attn_w2': _L0_attn_in['w2'], 'L0_attn_b2': _L0_attn_in['b2'], 'L0_attn_ln1_g': _L0_attn_in['ln1_g'], 'L0_attn_ln1_b': _L0_attn_in['ln1_b'], 'L0_attn_ln2_g': _L0_attn_in['ln2_g'], 'L0_attn_ln2_b': _L0_attn_in['ln2_b'], 'L0_ffn_W_r': _L0_ffn_in['W_r'], 'L0_ffn_W_k': _L0_ffn_in['W_k'], 'L0_ffn_W_v': _L0_ffn_in['W_v'], 'L0_ffn_mu_r': _L0_ffn_in['mu_r'], 'L0_ffn_mu_k': _L0_ffn_in['mu_k']}
    _x0 = _d['L0_attn_x']
    _d['L0_attn_x'] = jax.random.normal(jax.random.fold_in(jax.random.key(seed), 1), (32, 256, 128), dtype=_x0.dtype)
    del _x0
    return _d

def reference(L0_attn_x, L0_attn_rel_pos, L0_attn_in_proj_w, L0_attn_in_proj_b, L0_attn_out_w, L0_attn_out_b, L0_attn_w1, L0_attn_b1, L0_attn_w2, L0_attn_b2, L0_attn_ln1_g, L0_attn_ln1_b, L0_attn_ln2_g, L0_attn_ln2_b, L0_ffn_W_r, L0_ffn_W_k, L0_ffn_W_v, L0_ffn_mu_r, L0_ffn_mu_k):

    def _L0_attn_ref(x, rel_pos, in_proj_w, in_proj_b, out_w, out_b, w1, b1, w2, b2, ln1_g, ln1_b, ln2_g, ln2_b):
        import jax, jax.numpy as jnp
        import numpy as np
        B, S, E, H, ML = (4, 128, 128, 16, 256)
        HD = E // H

        def _layernorm(x, g, b, eps=1e-05):
            m = x.mean(-1, keepdims=True)
            v = ((x - m) ** 2).mean(-1, keepdims=True)
            return (x - m) * jax.lax.rsqrt(v + eps) * g + b

        def _causal_mask(size, rel_pos):
            flipped = jnp.flip(rel_pos[:, :size], -1)
            neg_inf = jnp.full((rel_pos.shape[0], size), -jnp.inf, rel_pos.dtype)
            padded = jnp.concatenate([flipped, neg_inf], axis=-1)
            idx = jnp.arange(size)[None, :] - jnp.arange(size)[:, None] + size - 1
            return padded[:, idx]
        b, s, e = x.shape
        xn = _layernorm(x, ln1_g, ln1_b)
        qkv = xn @ in_proj_w.T + in_proj_b
        q, k, v = jnp.split(qkv, 3, axis=-1)
        q = q.reshape(b, s, H, HD).transpose(0, 2, 1, 3)
        k = k.reshape(b, s, H, HD).transpose(0, 2, 1, 3)
        v = v.reshape(b, s, H, HD).transpose(0, 2, 1, 3)
        mask = _causal_mask(s, rel_pos)
        scores = jnp.einsum('bhqd,bhkd->bhqk', q, k) / np.sqrt(HD) + mask[None]
        attn = jax.nn.softmax(scores, axis=-1)
        o = jnp.einsum('bhqk,bhkd->bhqd', attn, v)
        o = o.transpose(0, 2, 1, 3).reshape(b, s, e)
        att_out = o @ out_w.T + out_b
        x = x + att_out
        xm = _layernorm(x, ln2_g, ln2_b)
        mlp = jax.nn.relu(xm @ w1.T + b1) @ w2.T + b2
        return x + mlp

    def _L0_ffn_ref(x, W_r, W_k, W_v, mu_r, mu_k):
        import jax, jax.numpy as jnp
        import numpy as np
        DIM = 128

        def _reference_tuple_inner(x, W_r, W_k, W_v, mu_r, mu_k):
            B, T, C = x.shape
            x_prev = jnp.concatenate([jnp.zeros((B, 1, C), x.dtype), x[:, :-1, :]], axis=1)
            xr = mu_r * x + (1.0 - mu_r) * x_prev
            xk = mu_k * x + (1.0 - mu_k) * x_prev
            r = jax.nn.sigmoid(jnp.einsum('btc,dc->btd', xr, W_r))
            k = jnp.einsum('btc,dc->btd', xk, W_k)
            k_act = jnp.square(jax.nn.relu(k))
            out = r * jnp.einsum('btc,dc->btd', k_act, W_v)
            new_state = x[:, -1, :]
            return (out, new_state)
        return _reference_tuple_inner(x, W_r, W_k, W_v, mu_r, mu_k)[0]
    x = L0_attn_x
    xn = _layernorm(x, axis=-1)
    s = _L0_attn_ref(xn, L0_attn_rel_pos, L0_attn_in_proj_w, L0_attn_in_proj_b, L0_attn_out_w, L0_attn_out_b, L0_attn_w1, L0_attn_b1, L0_attn_w2, L0_attn_b2, L0_attn_ln1_g, L0_attn_ln1_b, L0_attn_ln2_g, L0_attn_ln2_b)
    g = _silu(_L0_ffn_ref(xn, L0_ffn_W_r, L0_ffn_W_k, L0_ffn_W_v, L0_ffn_mu_r, L0_ffn_mu_k))
    x = x + s * g
    return x

_drawn_inputs = setup_inputs


def setup_inputs(seed=0):
    import zlib

    import numpy as np

    out = dict(_drawn_inputs(seed))
    spreads = {'L0_attn_in_proj_b': (0.0, 0.8),
     'L0_attn_out_b': (0.0, 0.8),
     'L0_attn_b1': (0.0, 0.8),
     'L0_attn_b2': (0.0, 0.8),
     'L0_attn_ln1_g': (1.0, 0.6),
     'L0_attn_ln1_b': (0.0, 0.8),
     'L0_attn_ln2_g': (1.0, 0.6),
     'L0_attn_ln2_b': (0.0, 0.8)}
    factors = {'L0_attn_rel_pos': 8.0,
     'L0_attn_in_proj_w': 8.0,
     'L0_attn_out_w': 8.0,
     'L0_attn_w1': 8.0,
     'L0_attn_w2': 8.0,
     'L0_ffn_W_r': 6.229,
     'L0_ffn_mu_r': 8.0}
    for name, (base, spread) in spreads.items():
        noise = np.random.default_rng([zlib.crc32(name.encode()), seed]).standard_normal(out[name].shape)
        drawn = base * np.exp(spread * noise) if base else spread * noise
        out[name] = jnp.asarray(drawn.astype(out[name].dtype))
    for name, factor in factors.items():
        out[name] = (out[name] * factor).astype(out[name].dtype)
    return out
```

```python
from contextlib import ExitStack

import numpy as np

import concourse.bass as bass
from concourse import mybir

BATCHES, SEQ, EMB, HEADS = 32, 256, 128, 16
HEAD_DIM = EMB // HEADS
TILE = 128
TT = SEQ // TILE
HIDDEN = 4 * EMB
FT = HIDDEN // TILE
EPS = 1e-5
MASKED = -1e30
QSCALE = HEAD_DIM ** -0.5

Q_ROWS = ((0, 3), (0, 2), (0, 1))
K_ROWS = ((0, 1), (0, 1), (0, 1), (1, 2), (1, 2), (2, 3))
STACK_DMAS = 16 * (len(Q_ROWS) + len(K_ROWS))
PAIR_ROWS = 6 * HEAD_DIM
A_ROWS = 96
M_ROW = 96
B_ROWS = M_ROW + 2
HALF = HEADS // 2
GROUP = 4
GROUPS = HEADS // GROUP
UNITS = 3 * GROUPS
UNROLL = 4

C_WQKV = 0
C_WO = C_WQKV + 3 * EMB
C_W1 = C_WO + EMB
C_W2 = C_W1 + HIDDEN
C_WR = C_W2 + HIDDEN
C_WK = C_WR + EMB
C_WV = C_WK + EMB
C_ID = C_WV + EMB
C_BV = C_ID + EMB
C_BO = C_BV + EMB
C_B2 = C_BO + EMB
C_BQ = C_B2 + EMB
C_BK = C_BQ + 1
C_B1 = C_BK + 1
C_G1 = C_B1 + FT
C_L1 = C_G1 + 1
C_G2 = C_L1 + 1
C_L2 = C_G2 + 1
C_MR = C_L2 + 1
C_MK = C_MR + 1
C_ALL = C_MK + 1

F32 = mybir.dt.float32
F32R = mybir.dt.float32r
BF16 = mybir.dt.bfloat16
ALU = mybir.AluOpType
ACT = mybir.ActivationFunctionType


class Batch:

    def __init__(self, first, turn=None):
        self.first, self.turn = first, turn

    def minus(self, n):
        return Batch(self.first - n, self.turn)

    def live(self):
        return self.turn is not None or 0 <= self.first < BATCHES

    def index(self):
        return self.first if self.turn is None else self.turn * UNROLL + self.first

    def slot(self, n):
        return self.first % n


def count(per, b, extra):
    n = per * b.first + extra
    assert b.turn is None or n > 0, "a wait in the loop must be above zero"
    return n if b.turn is None else b.turn * (UNROLL * per) + n


def count2(per, b, extra):
    n = per * (b.first // 2) + extra
    assert b.turn is None or n > 0, "a wait in the loop must be above zero"
    return n if b.turn is None else b.turn * (UNROLL // 2 * per) + n


def wait(eng, sem, value):
    if isinstance(value, int) and value <= 0:
        return
    eng.wait_ge(sem, value)


def group_heads(grp):
    return [grp // 2 * HALF + 2 * j + grp % 2 for j in range(GROUP)]


def hold(eng, passed):
    eng.sem_inc(passed, 1)


def each_step(eng, body):
    for s in range(-1, 3):
        body(Batch(s))
    with eng.Fori(0, 7) as turn:
        for k in range(UNROLL):
            body(Batch(3 + k, turn))
    for s in range(31, BATCHES + 3):
        body(Batch(s))


def stages(s):
    return [s.minus(n) for n in (-1, 0, 1, 1, 2, 2, 3)]


JOBS = [("max1", 0, 2), ("xT", 1, 0), ("oT", 0, 3), ("qk", 1, 0), ("onT", 0, 3), ("att", 1, 3),
        ("v", 0, 0), ("max0", 1, 1), ("k", 0, 0), ("x2T", 1, 3), ("up0", 0, 3), ("up1", 1, 3),
        ("down", 0, 3), ("r", 1, 0), ("y", 0, 0)]


def gated_block(nc, x, consts, rel_kq, rel_qk, out):
    parts_dram = nc.dram_tensor("parts_dram", (2, 3, HEAD_DIM, HEADS, 2 * SEQ), BF16).ap()
    max_dram = nc.dram_tensor("max_dram", (2, 2, 2, HALF * TT * TILE), BF16).ap()

    with ExitStack() as ctx:
        def sb(name, shape, dt=F32):
            return ctx.enter_context(nc.sbuf_tensor(name, shape, dt))

        def pb(name, shape, dt=F32):
            return ctx.enter_context(nc.psum_tensor(name, shape, dt))

        def sem(name):
            return ctx.enter_context(nc.semaphore(name))

        cst = sb("cst", [128, C_ALL])
        ident = cst[:, C_ID:C_ID + EMB]
        identb = sb("identb", [128, 128], BF16)
        identr = sb("identr", [128, 128], F32R)
        bqs = sb("bqs", [128, 1])
        neghalf = sb("neghalf", [128, TT])
        relA = sb("relA", [128, HEADS, SEQ])
        relB = sb("relB", [128, HEADS, SEQ])
        relBh = sb("relBh", [128, HEADS, SEQ], F32R)
        relBl = sb("relBl", [128, HEADS, SEQ], F32R)

        xin = sb("xin", [128, 2, TT, EMB])
        stats = sb("stats", [128, TT, 6])
        mv = sb("mv", [128, TT, 2])
        lnv = sb("lnv", [128, 8, TT])
        xn0 = sb("xn0", [128, 4, TT, EMB])
        xh = sb("xh", [128, 2, TT, EMB])
        xn0T = sb("xn0T", [128, 2, SEQ + 1])
        xn1T = sb("xn1T", [128, 2, SEQ])
        dx = sb("dx", [128, SEQ])
        xrT = sb("xrT", [128, SEQ])
        xkT = sb("xkT", [128, SEQ])
        qk32 = sb("qk32", [128, 2 * SEQ])
        rest = sb("rest", [128, 2 * SEQ])
        parts = sb("parts", [128, 2, 3, 2 * SEQ], BF16)
        vst = sb("vst", [128, 4, TT, HEADS, 32])
        krelu = sb("krelu", [128, SEQ])
        kact = sb("kact", [128, SEQ])
        thr = sb("thr", [128, SEQ])
        y2 = sb("y2", [128, SEQ])
        thy = sb("thy", [128, SEQ])
        gate = sb("gate", [128, 4, SEQ])
        qst = sb("qst", [128, 2, HEADS, SEQ], BF16)
        kst = sb("kst", [128, 2, HEADS, SEQ], BF16)
        mx = sb("mx", [128, HEADS, TT])
        mparts = sb("mparts", [128, 2, 2, HALF * TT], BF16)
        maxT = sb("maxT", [2 * HALF * TT, 2, TILE], BF16)
        prob = sb("prob", [128, 6, 512])
        osb = sb("osb", [128, 512])
        rsum = sb("rsum", [128, TT * HEADS])
        on = sb("on", [128, TT * EMB])
        onT = sb("onT", [128, SEQ])
        xb = sb("xb", [128, TT, EMB])
        x1 = sb("x1", [128, TT, EMB])
        x1b = sb("x1b", [128, TT, EMB])
        stats2 = sb("stats2", [128, TT, 6])
        mv2 = sb("mv2", [128, TT, 2])
        lnv2 = sb("lnv2", [128, 3, TT])
        xh2 = sb("xh2", [128, TT, EMB])
        xmT = sb("xmT", [128, SEQ])
        hT = sb("hT", [128, FT, SEQ])
        s1 = sb("s1", [128, SEQ])
        s2 = sb("s2", [128, SEQ])
        xc = sb("xc", [128, 2, TT, EMB])
        yo = sb("yo", [128, 2, TT, EMB])

        psA = [pb(f"psA{i}", [128, 512]) for i in range(2)]
        psB = [pb(f"psB{i}", [128, 512]) for i in range(3)]
        psO = pb("psO", [128, 512])
        psP = [pb(f"psP{i}", [128, 512]) for i in range(2)]

        s_cst = sem("s_cst")
        s_passd, s_passp, s_passs = sem("s_passd"), sem("s_passp"), sem("s_passs")
        s_rel = sem("s_rel")
        s_init = sem("s_init")
        s_initp = sem("s_initp")
        s_xin = [sem(f"s_xin{i}") for i in range(2)]
        s_stats = sem("s_stats")
        s_mv = sem("s_mv")
        s_ln = sem("s_ln")
        s_initv = sem("s_initv")
        s_xa = sem("s_xa")
        s_xn = sem("s_xn")
        s_xTps = sem("s_xTps")
        s_xT = sem("s_xT")
        s_dx = sem("s_dx")
        s_xrk = sem("s_xrk")
        s_qkps = sem("s_qkps")
        s_qkhi = sem("s_qkhi")
        s_rest = sem("s_rest")
        s_mid = sem("s_mid")
        s_low = sem("s_low")
        s_pout = sem("s_pout")
        s_st = [[sem(f"s_st{i}{h}") for h in range(2)] for i in range(2)]
        s_vps = sem("s_vps")
        s_v = sem("s_v")
        s_kps = sem("s_kps")
        s_krelu = sem("s_krelu")
        s_kact = sem("s_kact")
        s_rps = sem("s_rps")
        s_thr = sem("s_thr")
        s_yps = sem("s_yps")
        s_y2 = sem("s_y2")
        s_thy = sem("s_thy")
        s_gate = sem("s_gate")
        s_sA = sem("s_sA")
        s_ttr = sem("s_ttr")
        s_mhi = sem("s_mhi")
        s_mp = sem("s_mp")
        s_mps = [sem(f"s_mps{h}") for h in range(2)]
        s_mT = [sem(f"s_mT{h}") for h in range(2)]
        s_mout = [sem(f"s_mout{h}") for h in range(2)]
        s_min = [[sem(f"s_min{i}{h}") for h in range(2)] for i in range(2)]
        s_sB = sem("s_sB")
        s_exp = sem("s_exp")
        s_pv = sem("s_pv")
        s_osb = sem("s_osb")
        s_oTps = sem("s_oTps")
        s_rsum = sem("s_rsum")
        s_on = sem("s_on")
        s_onTps = sem("s_onTps")
        s_onT = sem("s_onT")
        s_attps = sem("s_attps")
        s_xb = sem("s_xb")
        s_x1 = sem("s_x1")
        s_st2 = sem("s_st2")
        s_mv2 = sem("s_mv2")
        s_ln2 = sem("s_ln2")
        s_xh2 = sem("s_xh2")
        s_x1b = sem("s_x1b")
        s_x2Tps = sem("s_x2Tps")
        s_xmT = sem("s_xmT")
        s_upps = sem("s_upps")
        s_h = sem("s_h")
        s_dnps = sem("s_dnps")
        s_s1 = sem("s_s1")
        s_s2 = sem("s_s2")
        s_xc = [sem(f"s_xc{i}") for i in range(2)]
        s_yo = sem("s_yo")
        s_out = [sem(f"s_out{i}") for i in range(2)]

        FREED = {"max1": (s_mT[1], 1, 1), "xT": (s_xT, 1, 1), "oT": (s_on, 1, 1), "qk": (s_qkhi, 1, 1),
                 "onT": (s_onT, 1, 1), "att": (s_x1, 1, 1), "v": (s_v, 1, 1), "max0": (s_mT[0], 1, 1),
                 "k": (s_krelu, 1, 1), "x2T": (s_xmT, 1, 1), "up0": (s_h, 2, 1), "up1": (s_h, 2, 2),
                 "down": (s_s1, 1, 1), "r": (s_thr, 1, 1), "y": (s_y2, 1, 1)}

        def bank_free(eng, name, s):
            at = [j[0] for j in JOBS].index(name)
            back = [(j, 0) for j in JOBS[:at][::-1]] + [(j, n) for n in range(1, 4) for j in JOBS[::-1]]
            for (other, bank, lag), steps in back:
                b = s.minus(lag + steps)
                if bank == JOBS[at][1] and b.live():
                    done, per, which = FREED[other]
                    wait(eng, done, count(per, b, which))
                    return

        def col(c):
            return cst[:, c:c + 1]

        def spread(c):
            return cst[:, c:c + EMB].unsqueeze(1).to_broadcast([128, TT, EMB])

        block = ctx.enter_context(nc.Block())

        @block.sync
        def _(sp):
            xv = x.rearrange("b (t p) e -> b p t e", p=TILE)
            ov = out.rearrange("b (t p) e -> b p t e", p=TILE)
            sp.dma_start(xin[:, 0], xv[0]).then_inc(s_xin[0], 16)
            sp.dma_start(cst[:], consts).then_inc(s_cst, 16)
            sp.dma_start(relA[:], rel_qk).then_inc(s_rel, 16)
            sp.dma_start(relB[:], rel_kq).then_inc(s_rel, 16)

            def stack_half(b, h):
                p = b.slot(2)
                heads = slice(h * HALF, h * HALF + HALF)
                sp.wait_ge(s_pout, count(48, b, 48))
                hold(sp, s_passs)
                wait(sp, s_sB, count(12, b.minus(2), 6 * h + 6))
                if h == 0:
                    wait(sp, s_init, 1 if b.first < 2 and b.turn is None else 0)
                for tile, rows, at in ((qst, Q_ROWS, 0), (kst, K_ROWS, SEQ)):
                    row = 0
                    for first, last in rows:
                        n = (last - first) * HEAD_DIM
                        src = parts_dram[p, first:last, :, heads, at:at + SEQ].rearrange("c d h q -> (c d) h q")
                        sp.dma_start(tile[row:row + n, p, heads, :], src).then_inc(s_st[p][h], 16)
                        row += n

            def max_half(b, h):
                p = b.slot(2)
                dst = max_dram[p, h].rearrange("c (n q) -> (c n) q", q=TILE)
                sp.wait_ge(s_mT[h], count(1, b, 1))
                sp.dma_start(dst, maxT[:, h, :]).then_inc(s_mout[h], 16)
                sp.wait_ge(s_mout[h], count(16, b, 16))
                sp.dma_start(qst[M_ROW:M_ROW + 2, p, h * HALF:(h + 1) * HALF, :],
                             max_dram[p, h].rearrange("c (h q) -> c h q", q=SEQ)).then_inc(s_min[p][h], 16)

            def step(s):
                n, f, g, a, a1, b, c = stages(s)
                if n.live() and (n.first > 0 or n.turn is not None):
                    wait(sp, s_xn, count(1, n, -1))
                    hold(sp, s_passs)
                    sp.dma_start(xin[:, n.slot(2)], xv[n.index()]).then_inc(s_xin[n.slot(2)], 16)
                if a1.live():
                    max_half(a1, 1)
                if c.live():
                    sp.dma_start(xc[:, c.slot(2)], xv[c.index()]).then_inc(s_xc[c.slot(2)], 16)
                if a.live():
                    max_half(a, 0)
                if f.live():
                    p = f.slot(2)
                    sp.wait_ge(s_low, count(1, f, 1))
                    hold(sp, s_passs)
                    wait(sp, s_st[p][1], count2(STACK_DMAS, f, 0))
                    for c3 in range(3):
                        sp.dma_start(parts_dram[p, c3].rearrange("d h q -> h d q"),
                                     parts[:, p, c3]).then_inc(s_pout, 16)
                    stack_half(f, 0)
                if c.live():
                    sp.wait_ge(s_yo, count(1, c, 1))
                    hold(sp, s_passs)
                    sp.dma_start(ov[c.index()], yo[:, c.slot(2)]).then_inc(s_out[c.slot(2)], 16)
                if f.live():
                    stack_half(f, 1)
                if c.live():
                    sp.wait_ge(s_out[c.slot(2)], count2(16, c, 16))
                    hold(sp, s_passs)

            each_step(sp, step)
            for o in s_out:
                sp.wait_ge(o, 16 * BATCHES // 2)

        @block.gpsimd
        def _(pool):
            nc.gpsimd.memset(neghalf[:], -0.5).then_inc(s_initp, 1)
            nc.gpsimd.memset(xn0T[:, :, 0:1], 0.0).then_inc(s_initp, 1)

            def step(s):
                n, f, g, a, a1, b, c = stages(s)
                if c.live():
                    pool.wait_ge(s_cst, 16)
                    nc.gpsimd.tensor_tensor(xb[:], xn0[:, c.slot(4)], spread(C_BO), ALU.add).then_inc(s_xb, 1)
                if f.live():
                    p = f.slot(2)
                    pool.wait_ge(s_xT, count(1, f, 1))
                    wait(pool, s_xrk, count(1, f, 0))
                    nc.gpsimd.tensor_tensor(dx[:], xn0T[:, p, 1:SEQ + 1], xn0T[:, p, 0:SEQ],
                                            ALU.subtract).then_inc(s_dx, 1)
                    pool.wait_ge(s_qkhi, count(1, f, 1))
                    nc.gpsimd.tensor_tensor(rest[:], qk32[:], parts[:, p, 0], ALU.subtract).then_inc(s_rest, 1)
                    pool.wait_ge(s_mid, count(1, f, 1))
                    nc.gpsimd.tensor_tensor(parts[:, p, 2], rest[:], parts[:, p, 1],
                                            ALU.subtract).then_inc(s_low, 1)
                if c.live():
                    pool.wait_ge(s_mv2, count(1, c, 1))
                    hold(pool, s_passp)
                    nc.gpsimd.tensor_scalar(lnv2[:, 0], mv2[:, :, 0], -1.0, 1.0, ALU.mult,
                                            ALU.mult).then_inc(s_ln2, 1)
                    nc.gpsimd.tensor_scalar(lnv2[:, 1], mv2[:, :, 1], EPS, 1.0, ALU.add,
                                            ALU.mult).then_inc(s_ln2, 1)
                    pool.wait_ge(s_ln2, count(3, c, 2))
                    nc.gpsimd.tensor_tensor(lnv2[:, 2], lnv2[:, 1], neghalf[:], ALU.pow).then_inc(s_ln2, 1)
                    pool.wait_ge(s_ln2, count(3, c, 3))
                    hold(pool, s_passp)
                    for t in range(TT):
                        ins = nc.gpsimd.tensor_scalar(xh2[:, t], x1[:, t], lnv2[:, 0, t:t + 1],
                                                      lnv2[:, 2, t:t + 1], ALU.add, ALU.mult)
                    ins.then_inc(s_xh2, 1)
                    nc.gpsimd.tensor_tensor(x1b[:], x1[:], spread(C_B2), ALU.add).then_inc(s_x1b, 1)
                if f.live():
                    pool.wait_ge(s_krelu, count(1, f, 1))
                    wait(pool, s_yps, count(1, f, 0))
                    nc.gpsimd.tensor_tensor(kact[:], krelu[:], krelu[:], ALU.mult).then_inc(s_kact, 1)
                if n.live():
                    pool.wait_ge(s_mv, count(1, n, 1))
                    nm, a0, rs0, v1, v2, a1_, rs1 = [lnv[:, i] for i in range(7)]
                    v = mv[:, :, 1]
                    hold(pool, s_passp)
                    nc.gpsimd.tensor_scalar(nm, mv[:, :, 0], -1.0, 1.0, ALU.mult, ALU.mult).then_inc(s_ln, 1)
                    nc.gpsimd.tensor_scalar(a0, v, EPS, 1.0, ALU.add, ALU.mult).then_inc(s_ln, 1)
                    pool.wait_ge(s_ln, count(7, n, 2))
                    nc.gpsimd.tensor_tensor(rs0, a0, neghalf[:], ALU.pow).then_inc(s_ln, 1)
                    pool.wait_ge(s_ln, count(7, n, 3))
                    nc.gpsimd.tensor_tensor(v1, v, rs0, ALU.mult).then_inc(s_ln, 1)
                    pool.wait_ge(s_ln, count(7, n, 4))
                    nc.gpsimd.tensor_tensor(v2, v1, rs0, ALU.mult).then_inc(s_ln, 1)
                    pool.wait_ge(s_ln, count(7, n, 5))
                    hold(pool, s_passp)
                    nc.gpsimd.tensor_scalar(a1_, v2, EPS, 1.0, ALU.add, ALU.mult).then_inc(s_ln, 1)
                    pool.wait_ge(s_ln, count(7, n, 6))
                    nc.gpsimd.tensor_tensor(rs1, a1_, neghalf[:], ALU.pow).then_inc(s_ln, 1)
                    for t in range(TT):
                        ins = nc.gpsimd.tensor_scalar(xn0[:, n.slot(4), t], xin[:, n.slot(2), t], nm[:, t:t + 1],
                                                      rs0[:, t:t + 1], ALU.add, ALU.mult)
                        ins.then_inc(s_xa, 1)
                    pool.wait_ge(s_ln, count(7, n, 7))
                    pool.wait_ge(s_xa, count(2, n, 2))
                    hold(pool, s_passp)
                    for t in range(TT):
                        ins = nc.gpsimd.tensor_scalar(xh[:, n.slot(2), t], xn0[:, n.slot(4), t], rs1[:, t:t + 1],
                                                      1.0, ALU.mult, ALU.mult)
                    ins.then_inc(s_xn, 1)
                if c.live():
                    pool.wait_ge(s_s2, count(1, c, 1))
                    pool.wait_ge(s_xc[c.slot(2)], count2(16, c, 16))
                    nc.gpsimd.tensor_tensor(yo[:, c.slot(2)], s2[:].rearrange("p (t e) -> p t e", t=TT),
                                            xc[:, c.slot(2)], ALU.add).then_inc(s_yo, 1)

            each_step(pool, step)

        @block.scalar
        def _(act):
            def exp_unit(b, u):
                act.wait_ge(s_sB, count(12, b, u + 1))
                wait(act, s_pv, count(4, b, u // 3 - 1))
                nc.scalar.activation(prob[:, u % 6], psB[u % 3][:], ACT.Exp).then_inc(s_exp, 1)

            def turned_max(b, h):
                bank = psP[1 - h]
                act.wait_ge(s_mps[h], count(1, b, 1))
                wait(act, s_mout[h], count(16, b, 0))
                nc.scalar.activation(maxT[:, h, :], bank[0:2 * HALF * TT, 0:TILE // 2].bitcast(BF16),
                                     ACT.Copy).then_inc(s_mT[h], 1)

            def step(s):
                n, f, g, a, a1, b, c = stages(s)
                if s.first == 0 and s.turn is None:
                    act.wait_ge(s_cst, 16)
                    act.wait_ge(s_init, 1)
                    act.wait_ge(s_initp, 2)
                if g.live():
                    act.wait_ge(s_y2, count(1, g, 1))
                    wait(act, s_gate, count(1, g, 0))
                    nc.scalar.activation(thy[:], y2[:], ACT.Tanh, scale=0.25).then_inc(s_thy, 1)
                if b.live():
                    exp_unit(b, 0)
                if a1.live():
                    turned_max(a1, 1)
                if b.live():
                    exp_unit(b, 1)
                if f.live():
                    p = f.slot(2)
                    act.wait_ge(s_xTps, count(1, f, 1))
                    wait(act, s_xrk, count(1, f, -1))
                    wait(act, s_dx, count(1, f, -1))
                    nc.scalar.activation(xn0T[:, p, 1:SEQ + 1], psP[1][:, 0:SEQ], ACT.Copy)
                    nc.scalar.activation(xn1T[:, p], psP[1][:, SEQ:2 * SEQ], ACT.Identity, scale=col(C_G1),
                                         bias=col(C_L1)).then_inc(s_xT, 1)
                if c.live():
                    act.wait_ge(s_pv, count(4, c, 4))
                    nc.scalar.activation(osb[:], psO[:], ACT.Copy).then_inc(s_osb, 1)
                if b.live():
                    exp_unit(b, 2)
                if f.live():
                    act.wait_ge(s_qkps, count(1, f, 1))
                    wait(act, s_rest, count(1, f, 0))
                    wait(act, s_pout, count(48, f.minus(1), 0))
                    for dst in (qk32[:], parts[:, p, 0]):
                        nc.scalar.activation(dst[:, 0:SEQ], psP[1][:, 0:SEQ], ACT.Identity, scale=QSCALE,
                                             bias=bqs[:])
                        ins = nc.scalar.activation(dst[:, SEQ:2 * SEQ], psP[1][:, SEQ:2 * SEQ], ACT.Identity,
                                                   bias=col(C_BK))
                    ins.then_inc(s_qkhi, 1)
                if b.live():
                    exp_unit(b, 3)
                if c.live():
                    act.wait_ge(s_onTps, count(1, c, 1))
                    nc.scalar.activation(onT[:], psP[0][:, 0:SEQ], ACT.Copy).then_inc(s_onT, 1)
                if b.live():
                    exp_unit(b, 4)
                if f.live():
                    act.wait_ge(s_rest, count(1, f, 1))
                    nc.scalar.activation(parts[:, p, 1], rest[:], ACT.Copy).then_inc(s_mid, 1)
                if b.live():
                    exp_unit(b, 5)
                    exp_unit(b, 6)
                if a.live():
                    turned_max(a, 0)
                if b.live():
                    exp_unit(b, 7)
                if f.live():
                    act.wait_ge(s_kps, count(1, f, 1))
                    wait(act, s_kact, count(1, f, 0))
                    nc.scalar.activation(krelu[:], psP[0][:, 0:SEQ], ACT.Relu).then_inc(s_krelu, 1)
                if c.live():
                    act.wait_ge(s_x2Tps, count(1, c, 1))
                    nc.scalar.activation(xmT[:], psP[1][:, 0:SEQ], ACT.Identity, scale=col(C_G2),
                                         bias=col(C_L2)).then_inc(s_xmT, 1)
                if b.live():
                    exp_unit(b, 8)
                    exp_unit(b, 9)
                for i in range(2):
                    if c.live():
                        act.wait_ge(s_upps, count(2, c, i + 1))
                        for j in range(2):
                            k = 2 * i + j
                            ins = nc.scalar.activation(hT[:, k], psP[i][:, j * SEQ:(j + 1) * SEQ], ACT.Relu,
                                                       bias=col(C_B1 + k))
                        ins.then_inc(s_h, 1)
                    if b.live():
                        exp_unit(b, 10 + i)
                if f.live():
                    act.wait_ge(s_rps, count(1, f, 1))
                    wait(act, s_y2, count(1, f, 0))
                    nc.scalar.activation(thr[:], psP[1][:, 0:SEQ], ACT.Tanh, scale=0.5).then_inc(s_thr, 1)

            each_step(act, step)

        @block.vector
        def _(dve):
            nc.vector.memset(qst[:], 0.0).then_inc(s_initv, 1)
            nc.vector.memset(kst[:], 0.0).then_inc(s_initv, 1)
            nc.vector.memset(vst[:], 0.0).then_inc(s_initv, 1)
            dve.wait_ge(s_initv, 3)
            nc.vector.memset(kst[M_ROW:M_ROW + 2], 1.0).then_inc(s_initv, 1)
            for gg in range(2):
                ones = vst[:].rearrange("p s t (m g) w -> p (s t m) g w", g=2)[:, :, gg, 16 + 8 * gg:17 + 8 * gg]
                nc.vector.memset(ones, 1.0).then_inc(s_initv, 1)
            dve.wait_ge(s_cst, 16)
            nc.vector.tensor_copy(identb[:], ident).then_inc(s_initv, 1)
            nc.vector.tensor_copy(identr[:], ident).then_inc(s_initv, 1)
            nc.vector.tensor_scalar(bqs[:], col(C_BQ), QSCALE, None, ALU.mult).then_inc(s_initv, 1)
            dve.wait_ge(s_initv, 9)
            dve.wait_ge(s_rel, 32)
            nc.vector.tensor_copy(relBh[:], relB[:]).then_inc(s_init, 1)

            def ttr(b, h):
                bank = psA[h % 2]
                dve.wait_ge(s_sA, count(16, b, h + 1))
                hold(dve, s_passd)
                for t in range(TT):
                    s = bank[:, 0:TILE] if t == 0 else bank[:, TILE:TILE + SEQ]
                    ins = nc.vector.tensor_tensor_reduce(
                        out=s, in0=s, in1=relA[:, h, SEQ - (t + 1) * TILE:SEQ], scale=1.0, scalar=MASKED,
                        op0=ALU.add, op1=ALU.max, accum_out=mx[:, h, t:t + 1])
                ins.then_inc(s_ttr, 1)

            def max_parts(b, h):
                m = mx[:, h * HALF:(h + 1) * HALF, :].rearrange("p h t -> p (h t)")
                dve.wait_ge(s_ttr, count(16, b, (h + 1) * HALF))
                wait(dve, s_mps[h], count(1, b, 0))
                nc.vector.tensor_scalar(mparts[:, h, 0], m, -1.0, None, ALU.mult).then_inc(s_mhi, 1)
                dve.wait_ge(s_mhi, count(2, b, h + 1))
                nc.vector.scalar_tensor_tensor(out=mparts[:, h, 1], in0=m, scalar=-1.0, in1=mparts[:, h, 0],
                                               op0=ALU.mult, op1=ALU.subtract).then_inc(s_mp, 1)

            def layer_stats(src, st, mvt, s_own, s_done, own_value):
                for t in range(TT):
                    ins = nc.vector.bn_stats(st[:, t], src[:, t])
                ins.then_inc(s_own, 1)
                dve.wait_ge(s_own, own_value)
                hold(dve, s_passd)
                for t in range(TT):
                    ins = nc.vector.bn_aggr(mvt[:, t], st[:, t])
                ins.then_inc(s_done, 1)

            def step(s):
                n, f, g, a, a1, b, c = stages(s)
                if s.first == 0 and s.turn is None:
                    dve.wait_ge(s_init, 1)
                    nc.vector.tensor_tensor(relBl[:], relB[:], relBh[:].bitcast(F32), ALU.subtract).then_inc(s_init, 1)

                def head(h):
                    if a.live():
                        ttr(a, h)
                head(0)
                head(1)
                if g.live():
                    dve.wait_ge(s_thy, count(1, g, 1))
                    nc.vector.scalar_tensor_tensor(out=gate[:, g.slot(4)], in0=thy[:], scalar=1.0, in1=y2[:],
                                                   op0=ALU.add, op1=ALU.mult).then_inc(s_gate, 1)
                head(2)
                head(3)
                head(4)
                if c.live():
                    o = psP[0][:].rearrange("p (m w) -> p m w", w=32)
                    sums = o[:, :, 16:32].rearrange("p m (g w) -> p m g w", g=2)[:, :, :, 0]
                    heads = o[:, :, 0:16].rearrange("p m (g w) -> p m g w", g=2)
                    dve.wait_ge(s_oTps, count(1, c, 1))
                    nc.vector.reciprocal(rsum[:].rearrange("p (m g) -> p m g", g=2), sums).then_inc(s_rsum, 1)
                    dve.wait_ge(s_rsum, count(1, c, 1))
                    nc.vector.tensor_tensor(
                        on[:].rearrange("p (m g w) -> p m g w", g=2, w=8), heads,
                        rsum[:].rearrange("p (m g) -> p m g", g=2).unsqueeze(3).to_broadcast([128, 16, 2, 8]),
                        ALU.mult).then_inc(s_on, 1)
                head(5)
                if f.live():
                    p = f.slot(2)
                    dve.wait_ge(s_dx, count(1, f, 1))
                    wait(dve, s_rps, count(1, f, 0))
                    prev = xn0T[:, p, 0:SEQ]
                    nc.vector.scalar_tensor_tensor(out=xkT[:], in0=dx[:], scalar=col(C_MK), in1=prev,
                                                   op0=ALU.mult, op1=ALU.add)
                    nc.vector.scalar_tensor_tensor(out=xrT[:], in0=dx[:], scalar=col(C_MR), in1=prev,
                                                   op0=ALU.mult, op1=ALU.add).then_inc(s_xrk, 1)
                head(6)
                head(7)
                if a.live():
                    max_parts(a, 0)
                if c.live():
                    dve.wait_ge(s_attps, count(1, c, 1))
                    dve.wait_ge(s_xb, count(1, c, 1))
                    nc.vector.tensor_tensor(x1[:], psP[1][:, 0:SEQ].rearrange("p (t e) -> p t e", t=TT), xb[:],
                                            ALU.add).then_inc(s_x1, 1)
                    dve.wait_ge(s_x1, count(1, c, 1))
                    layer_stats(x1, stats2, mv2, s_st2, s_mv2, count(1, c, 1))
                head(8)
                if f.live():
                    dve.wait_ge(s_vps, count(1, f, 1))
                    for t in range(TT):
                        dst = vst[:, f.slot(4), t].rearrange("p (m g) w -> p m (g w)", g=2)
                        dst = bass.AP(dst.tensor, dst.offset, [list(dst.ap[0]), [64, HEADS // 2], [40, 2], [1, 8]])
                        ins = nc.vector.tensor_tensor(
                            dst, psP[0][:, t * EMB:(t + 1) * EMB].rearrange("p (m g w) -> p m g w", g=2, w=8),
                            col_row(C_BV), ALU.add)
                    ins.then_inc(s_v, 1)
                head(9)
                head(10)
                head(11)
                if n.live():
                    dve.wait_ge(s_xin[n.slot(2)], count2(16, n, 16))
                    wait(dve, s_ln, count(7, n, 0))
                    layer_stats(xin[:, n.slot(2)], stats, mv, s_stats, s_mv, count(1, n, 1))
                head(12)
                head(13)
                head(14)
                if c.live():
                    dve.wait_ge(s_dnps, count(1, c, 1))
                    dve.wait_ge(s_x1b, count(1, c, 1))
                    nc.vector.tensor_tensor(s1[:], psP[0][:, 0:SEQ], x1b[:].rearrange("p t e -> p (t e)"),
                                            ALU.add).then_inc(s_s1, 1)
                    dve.wait_ge(s_s1, count(1, c, 1))
                    nc.vector.scalar_tensor_tensor(out=s2[:], in0=s1[:], scalar=0.25, in1=gate[:, c.slot(4)],
                                                   op0=ALU.mult, op1=ALU.mult).then_inc(s_s2, 1)
                head(15)
                if a.live():
                    max_parts(a, 1)
                if f.live():
                    dve.wait_ge(s_yps, count(1, f, 1))
                    dve.wait_ge(s_thr, count(1, f, 1))
                    nc.vector.scalar_tensor_tensor(out=y2[:], in0=thr[:], scalar=1.0, in1=psP[0][:, 0:SEQ],
                                                   op0=ALU.add, op1=ALU.mult).then_inc(s_y2, 1)

            def col_row(c):
                return cst[:, c:c + EMB].rearrange("p (m g w) -> p m g w", g=2, w=8)

            each_step(dve, step)

        @block.tensor
        def _(pe):
            def a_unit(b, h):
                p, bank = b.slot(2), psA[h % 2]
                if h % HALF == 0:
                    pe.wait_ge(s_st[p][h // HALF], count2(STACK_DMAS, b, STACK_DMAS))
                wait(pe, s_ttr, count(16, b, h - 1))
                nc.tensor.matmul(bank[:, 0:TILE], qst[0:A_ROWS, p, h, 0:TILE], kst[0:A_ROWS, p, h, 0:TILE],
                                 start=True, stop=True)
                nc.tensor.matmul(bank[:, TILE:TILE + SEQ], qst[0:A_ROWS, p, h, TILE:SEQ], kst[0:A_ROWS, p, h, :],
                                 start=True, stop=True).then_inc(s_sA, 1)

            def b_unit(b, u):
                p, grp, i = b.slot(2), u // 3, u % 3
                bank = psB[i]
                if u % 6 == 0:
                    pe.wait_ge(s_min[p][u // 6], count2(16, b, 16))
                wait(pe, s_exp, count(12, b, u - 2))
                heads, width = group_heads(grp), TILE
                if i < 2:
                    heads, width = heads[2 * i:2 * i + 2], SEQ
                for n, rel in enumerate((relBh, relBl)):
                    nc.tensor.matmul(bank[:], identr[:], rel[:, heads[0]:heads[-1] + 1:2, 0:width],
                                     start=(n == 0), stop=False, skip_group_check=True)
                keys = slice(0, TILE) if i < 2 else slice(TILE, SEQ)
                for j, h in enumerate(heads):
                    ins = nc.tensor.matmul(bank[:, j * width:(j + 1) * width], kst[0:B_ROWS, p, h, keys],
                                           qst[0:B_ROWS, p, h, SEQ - width:SEQ], start=False,
                                           stop=(j == len(heads) - 1), skip_group_check=True)
                ins.then_inc(s_sB, 1)

            def pv(b, grp):
                if grp == 0:
                    pe.wait_ge(s_v, count(1, b, 1))
                    wait(pe, s_osb, count(1, b, 0))
                pe.wait_ge(s_exp, count(12, b, 3 * grp + 3))
                u, gg = grp // 2, grp % 2
                for kt in range(TT):
                    for j in range(GROUP):
                        w = vst[:, b.slot(4), kt, group_heads(grp)[j], :]
                        if kt == 0:
                            o = psO[32 * j:32 * j + 32, u * SEQ:(u + 1) * SEQ]
                            pr = prob[:, 3 * gg + j // 2, (j % 2) * SEQ:(j % 2 + 1) * SEQ]
                        else:
                            o = psO[32 * j:32 * j + 32, u * SEQ + TILE:(u + 1) * SEQ]
                            pr = prob[:, 3 * gg + 2, j * TILE:(j + 1) * TILE]
                        ins = nc.tensor.matmul(o, w, pr, start=(gg == 0 and kt == 0), stop=(gg == 1 and kt == 1),
                                               skip_group_check=True)
                ins.then_inc(s_pv, 1)

            def turned_max(b, h):
                bank = psP[1 - h]
                pe.wait_ge(s_mp, count(2, b, h + 1))
                nc.tensor.transpose(bank[0:2 * HALF * TT, 0:TILE // 2].bitcast(BF16),
                                    mparts[:, h].rearrange("p c n -> p (c n)"), identb[:]).then_inc(s_mps[h], 1)

            def turn(dst, src):
                return nc.tensor.transpose(dst, src, ident)

            def job(name, s, b):
                if not b.live():
                    return
                bank_free(pe, name, s)
                P0, P1 = psP
                p = b.slot(2)
                if name == "max1":
                    turned_max(b, 1)
                elif name == "max0":
                    turned_max(b, 0)
                elif name == "xT":
                    pe.wait_ge(s_xn, count(1, b, 1))
                    for t in range(TT):
                        turn(P1[:, t * TILE:(t + 1) * TILE], xn0[:, b.slot(4), t])
                    for t in range(TT):
                        ins = turn(P1[:, SEQ + t * TILE:SEQ + (t + 1) * TILE], xh[:, p, t])
                    ins.then_inc(s_xTps, 1)
                elif name == "qk":
                    pe.wait_ge(s_xT, count(1, b, 1))
                    for i in range(2):
                        ins = nc.tensor.matmul(P1[:, i * SEQ:(i + 1) * SEQ],
                                               cst[:, C_WQKV + i * EMB:C_WQKV + (i + 1) * EMB], xn1T[:, p],
                                               start=True, stop=True)
                    ins.then_inc(s_qkps, 1)
                elif name == "v":
                    for t in range(TT):
                        ins = nc.tensor.matmul(P0[:, t * EMB:(t + 1) * EMB], xn1T[:, p, t * TILE:(t + 1) * TILE],
                                               cst[:, C_WQKV + 2 * EMB:C_WQKV + 3 * EMB], start=True, stop=True)
                    ins.then_inc(s_vps, 1)
                elif name == "k":
                    pe.wait_ge(s_xrk, count(1, b, 1))
                    nc.tensor.matmul(P0[:, 0:SEQ], cst[:, C_WK:C_WK + EMB], xkT[:], start=True,
                                     stop=True).then_inc(s_kps, 1)
                elif name == "r":
                    for t in range(TT):
                        ins = nc.tensor.matmul(P1[:, t * EMB:(t + 1) * EMB], xrT[:, t * TILE:(t + 1) * TILE],
                                               cst[:, C_WR:C_WR + EMB], start=True, stop=True)
                    ins.then_inc(s_rps, 1)
                elif name == "y":
                    pe.wait_ge(s_kact, count(1, b, 1))
                    for t in range(TT):
                        ins = nc.tensor.matmul(P0[:, t * EMB:(t + 1) * EMB], kact[:, t * TILE:(t + 1) * TILE],
                                               cst[:, C_WV:C_WV + EMB], start=True, stop=True)
                    ins.then_inc(s_yps, 1)
                elif name == "oT":
                    pe.wait_ge(s_osb, count(1, b, 1))
                    for t in range(TT):
                        for u in range(2):
                            ins = turn(P0[:, (2 * t + u) * TILE:(2 * t + u + 1) * TILE],
                                       osb[:, u * SEQ + t * TILE:u * SEQ + (t + 1) * TILE])
                    ins.then_inc(s_oTps, 1)
                elif name == "onT":
                    pe.wait_ge(s_on, count(1, b, 1))
                    for t in range(TT):
                        ins = turn(P0[:, t * TILE:(t + 1) * TILE], on[:, t * EMB:(t + 1) * EMB])
                    ins.then_inc(s_onTps, 1)
                elif name == "att":
                    pe.wait_ge(s_onT, count(1, b, 1))
                    for t in range(TT):
                        ins = nc.tensor.matmul(P1[:, t * EMB:(t + 1) * EMB], onT[:, t * TILE:(t + 1) * TILE],
                                               cst[:, C_WO:C_WO + EMB], start=True, stop=True)
                    ins.then_inc(s_attps, 1)
                elif name == "x2T":
                    pe.wait_ge(s_xh2, count(1, b, 1))
                    for t in range(TT):
                        ins = turn(P1[:, t * TILE:(t + 1) * TILE], xh2[:, t])
                    ins.then_inc(s_x2Tps, 1)
                elif name in ("up0", "up1"):
                    i = int(name[-1])
                    pe.wait_ge(s_xmT, count(1, b, 1))
                    for j in range(2):
                        k = 2 * i + j
                        ins = nc.tensor.matmul(psP[i][:, j * SEQ:(j + 1) * SEQ],
                                               cst[:, C_W1 + k * TILE:C_W1 + (k + 1) * TILE], xmT[:],
                                               start=True, stop=True)
                    ins.then_inc(s_upps, 1)
                elif name == "down":
                    pe.wait_ge(s_h, count(2, b, 2))
                    for t in range(TT):
                        for k in range(FT):
                            ins = nc.tensor.matmul(P0[:, t * EMB:(t + 1) * EMB], hT[:, k, t * TILE:(t + 1) * TILE],
                                                   cst[:, C_W2 + k * EMB:C_W2 + (k + 1) * EMB],
                                                   start=(k == 0), stop=(k == FT - 1))
                    ins.then_inc(s_dnps, 1)

            AT = {1: ["max1"], 3: ["xT"], 4: ["oT"], 5: ["qk"], 6: ["onT"], 7: ["att"], 8: ["v"], 9: ["max0"],
                  10: ["k"], 11: ["x2T"], 12: ["up0"], 13: ["up1"], 14: ["down"], 15: ["r", "y"]}
            LAGS = {name: lag for name, _, lag in JOBS}
            SLOTS_B = {4 * g + i: u for g in range(GROUPS) for i, u in ((0, 3 * g), (1, 3 * g + 1), (3, 3 * g + 2))}

            def step(s):
                n, f, g, a, a1, b, c = stages(s)
                if s.first == 0 and s.turn is None:
                    pe.wait_ge(s_cst, 16)
                    pe.wait_ge(s_init, 1)
                if s.first == 1 and s.turn is None:
                    pe.wait_ge(s_init, 2)
                for i in range(HEADS):
                    if a.live():
                        a_unit(a, i)
                    if i % 4 == 2:
                        if i == 2:
                            if c.live():
                                pv(c, GROUPS - 1)
                        elif b.live():
                            pv(b, i // 4 - 1)
                    elif b.live():
                        b_unit(b, SLOTS_B[i])
                    for name in AT.get(i, []):
                        job(name, s, s.minus(LAGS[name]))

            each_step(pe, step)


_OUT = (BATCHES, SEQ, EMB)


def kernel(**inputs):
    import concourse.bacc as _bacc
    from concourse.bass_utils import run_bass_kernel_spmd as _run

    a = {k: np.asarray(v) for k, v in inputs.items()}

    def t(w):
        return np.ascontiguousarray(w.T)

    def row(v):
        return np.tile(v[None, :], (128, 1))

    w2 = t(a["L0_attn_w2"]).reshape(FT, TILE, EMB).transpose(1, 0, 2).reshape(TILE, HIDDEN)
    bqkv = a["L0_attn_in_proj_b"].reshape(3, EMB)
    consts = np.concatenate([
        t(a["L0_attn_in_proj_w"]), t(a["L0_attn_out_w"]), t(a["L0_attn_w1"]), w2, t(a["L0_ffn_W_r"]), t(a["L0_ffn_W_k"]),
        t(a["L0_ffn_W_v"]), np.eye(128, dtype=np.float32), row(bqkv[2]), row(a["L0_attn_out_b"]),
        row(a["L0_attn_b2"]), bqkv[0][:, None], bqkv[1][:, None], t(a["L0_attn_b1"].reshape(FT, TILE)),
        a["L0_attn_ln1_g"][:, None], a["L0_attn_ln1_b"][:, None], a["L0_attn_ln2_g"][:, None],
        a["L0_attn_ln2_b"][:, None], a["L0_ffn_mu_r"][:, None], a["L0_ffn_mu_k"][:, None]], axis=1)
    rel = np.concatenate([np.full((HEADS, TILE), MASKED, np.float32), a["L0_attn_rel_pos"][:, :SEQ]], axis=1)
    i, j = np.arange(TILE)[:, None], np.arange(SEQ)[None, :]
    rel_kq = rel[:, TILE + j - i].transpose(1, 0, 2)
    rel_qk = rel[:, TILE + (SEQ - TILE) + i - j].transpose(1, 0, 2)

    nc = _bacc.Bacc("TRN2", target_bir_lowering=False, num_devices=1)
    arrays, args = {}, []
    for name, v in (("x", a["L0_attn_x"]), ("consts", consts), ("rel_kq", rel_kq), ("rel_qk", rel_qk)):
        arrays[f"in_{name}"] = np.ascontiguousarray(v)
        args.append(nc.dram_tensor(f"in_{name}", v.shape, F32, kind="ExternalInput").ap())
    args.append(nc.dram_tensor("out_0", _OUT, F32, kind="ExternalOutput").ap())
    gated_block(nc, *args)
    r = _run(nc, [arrays], core_ids=[0])
    return r.results[0]["out_0"]
```

```python
from contextlib import ExitStack

import numpy as np

import concourse.bass as bass
from concourse import mybir

BATCHES, SEQ, EMB, HEADS = 32, 256, 128, 16
HEAD_DIM = EMB // HEADS
TILE = 128
TT = SEQ // TILE
HIDDEN = 4 * EMB
FT = HIDDEN // TILE
EPS = 1e-5
MASKED = -1e30
QSCALE = HEAD_DIM ** -0.5

BLOCKS = 3
STACK_DMAS = 16 * 2 * BLOCKS
PAIR_ROWS = 6 * HEAD_DIM
A_ROWS = 96
M_ROW = 96
B_ROWS = M_ROW + 2
HALF = HEADS // 2
GROUP = 4
GROUPS = HEADS // GROUP
UNITS = 3 * GROUPS
UNIT_AT = {4 * g + i: 3 * g + i for g in range(GROUPS) for i in range(3)}
ADDED = (2, 5, 8, 11)
UNROLL = 4

C_WQKV = 0
C_WO = C_WQKV + 3 * EMB
C_W1 = C_WO + EMB
C_W2 = C_W1 + HIDDEN
C_WR = C_W2 + HIDDEN
C_WK = C_WR + EMB
C_WV = C_WK + EMB
C_ID = C_WV + EMB
C_BO = C_ID + EMB
C_B2 = C_BO + EMB
C_BQ = C_B2 + EMB
C_BK = C_BQ + 1
C_B1 = C_BK + 1
C_G1 = C_B1 + FT
C_L1 = C_G1 + 1
C_G2 = C_L1 + 1
C_L2 = C_G2 + 1
C_MR = C_L2 + 1
C_MK = C_MR + 1
C_BV = C_MK + 1
C_ALL = C_BV + 1

F32 = mybir.dt.float32
F32R = mybir.dt.float32r
BF16 = mybir.dt.bfloat16
ALU = mybir.AluOpType
ACT = mybir.ActivationFunctionType


def unit_heads(u):
    heads, i = group_heads(u // 3), u % 3
    return (heads[2 * i:2 * i + 2], SEQ) if i < 2 else (heads, TILE)


class Batch:

    def __init__(self, first, turn=None):
        self.first, self.turn = first, turn

    def minus(self, n):
        return Batch(self.first - n, self.turn)

    def live(self):
        return self.turn is not None or 0 <= self.first < BATCHES

    def index(self):
        return self.first if self.turn is None else self.turn * UNROLL + self.first

    def slot(self, n):
        return self.first % n


def count(per, b, extra):
    n = per * b.first + extra
    assert b.turn is None or n > 0, "a wait in the loop must be above zero"
    return n if b.turn is None else b.turn * (UNROLL * per) + n


def count2(per, b, extra):
    n = per * (b.first // 2) + extra
    assert b.turn is None or n > 0, "a wait in the loop must be above zero"
    return n if b.turn is None else b.turn * (UNROLL // 2 * per) + n


def wait(eng, sem, value):
    if isinstance(value, int) and value <= 0:
        return
    eng.wait_ge(sem, value)


def group_heads(grp):
    return [grp // 2 * HALF + 2 * j + grp % 2 for j in range(GROUP)]


def hold(eng, passed):
    eng.sem_inc(passed, 1)


def each_step(eng, body):
    for s in range(-1, 3):
        body(Batch(s))
    with eng.Fori(0, 7) as turn:
        for k in range(UNROLL):
            body(Batch(3 + k, turn))
    for s in range(31, BATCHES + 3):
        body(Batch(s))


def stages(s):
    return [s.minus(n) for n in (-1, 0, 1, 2, 3)]


JOBS = [("max1", 1, 2), ("xT", 0, 0), ("qk", 1, 0), ("oT", 0, 3), ("v", 1, 0), ("onT", 0, 3), ("k", 1, 0),
        ("att", 0, 3), ("max0", 1, 1), ("r", 0, 0), ("y", 1, 0), ("x2T", 0, 3), ("up0", 1, 3), ("up1", 0, 3),
        ("down", 1, 3)]
BANK = {name: bank for name, bank, _ in JOBS}


def gated_block(nc, x, consts, rel_kq, rel_qk, out):
    parts_dram = nc.dram_tensor("parts_dram", (2, 2, 3, HEAD_DIM, HEADS, SEQ), BF16).ap()
    max_dram = nc.dram_tensor("max_dram", (2, 2, 2, HALF * TT * TILE), BF16).ap()

    with ExitStack() as ctx:
        def sb(name, shape, dt=F32):
            return ctx.enter_context(nc.sbuf_tensor(name, shape, dt))

        def pb(name, shape, dt=F32):
            return ctx.enter_context(nc.psum_tensor(name, shape, dt))

        def sem(name):
            return ctx.enter_context(nc.semaphore(name))

        cst = sb("cst", [128, C_ALL])
        ident = cst[:, C_ID:C_ID + EMB]
        identb = sb("identb", [128, 128], BF16)
        identr = sb("identr", [128, 128], F32R)
        bqs = sb("bqs", [128, 1])
        neghalf = sb("neghalf", [128, TT])
        relA = sb("relA", [128, HEADS, SEQ])
        relB = sb("relB", [128, HEADS, SEQ])
        relBh = sb("relBh", [128, HEADS, SEQ], F32R)
        relBl = sb("relBl", [128, HEADS, SEQ], F32R)

        xin = sb("xin", [128, 2, TT, EMB])
        stats = sb("stats", [128, TT, 6])
        mv = sb("mv", [128, TT, 2])
        lnv = sb("lnv", [128, 8, TT])
        xn0 = sb("xn0", [128, 4, TT, EMB])
        xh = sb("xh", [128, 2, TT, EMB])
        xn0T = sb("xn0T", [128, 2, SEQ + 1])
        xn1T = sb("xn1T", [128, 2, SEQ])
        dx = sb("dx", [128, SEQ])
        xrT = sb("xrT", [128, SEQ])
        xkT = sb("xkT", [128, SEQ])
        qk32 = sb("qk32", [128, 2, SEQ])
        rest = sb("rest", [128, 2, SEQ])
        parts = sb("parts", [128, 2, 2, 3, SEQ], BF16)
        vst = sb("vst", [128, 4, TT, HEADS, 32])
        krelu = sb("krelu", [128, SEQ])
        kact = sb("kact", [128, SEQ])
        thr = sb("thr", [128, SEQ])
        y2 = sb("y2", [128, SEQ])
        thy = sb("thy", [128, SEQ])
        thq = sb("thq", [128, SEQ])
        gate = sb("gate", [128, 4, SEQ])
        qst = sb("qst", [128, 2, HEADS, SEQ], BF16)
        kst = sb("kst", [128, 2, HEADS, SEQ], BF16)
        mx = sb("mx", [128, HEADS, TT])
        mparts = sb("mparts", [128, 2, 2, HALF * TT], BF16)
        maxT = sb("maxT", [2 * HALF * TT, 2, TILE], BF16)
        prob = sb("prob", [128, 6, 512])
        osb = sb("osb", [128, 512])
        rsum = sb("rsum", [128, TT * HEADS])
        on = sb("on", [128, TT * EMB])
        onT = sb("onT", [128, SEQ])
        xb = sb("xb", [128, TT, EMB])
        x1 = sb("x1", [128, TT, EMB])
        x1b = sb("x1b", [128, TT, EMB])
        stats2 = sb("stats2", [128, TT, 6])
        mv2 = sb("mv2", [128, TT, 2])
        lnv2 = sb("lnv2", [128, 3, TT])
        xh2 = sb("xh2", [128, TT, EMB])
        xmT = sb("xmT", [128, SEQ])
        hT = sb("hT", [128, FT, SEQ])
        s1 = sb("s1", [128, SEQ])
        s2 = sb("s2", [128, SEQ])
        xc = sb("xc", [128, 2, TT, EMB])
        yo = sb("yo", [128, 2, TT, EMB])

        psA = [pb(f"psA{i}", [128, 512]) for i in range(2)]
        psB = [pb(f"psB{i}", [128, 512]) for i in range(3)]
        psO = pb("psO", [128, 512])
        psP = [pb(f"psP{i}", [128, 512]) for i in range(2)]

        s_cst = sem("s_cst")
        s_passd, s_passp, s_passs = sem("s_passd"), sem("s_passp"), sem("s_passs")
        s_rela, s_relb = sem("s_rela"), sem("s_relb")
        s_bqs = sem("s_bqs")
        s_relh = sem("s_relh")
        s_init = sem("s_init")
        s_initp = sem("s_initp")
        s_xin = [sem(f"s_xin{i}") for i in range(2)]
        s_stats = sem("s_stats")
        s_mv = sem("s_mv")
        s_ln = sem("s_ln")
        s_initv = sem("s_initv")
        s_xa = sem("s_xa")
        s_xn = sem("s_xn")
        s_xTps = sem("s_xTps")
        s_xT = sem("s_xT")
        s_dx = sem("s_dx")
        s_xrk = sem("s_xrk")
        s_qkps = sem("s_qkps")
        s_qkhi = sem("s_qkhi")
        s_rest = sem("s_rest")
        s_mid = sem("s_mid")
        s_low = sem("s_low")
        s_pout = sem("s_pout")
        s_st = [[sem(f"s_st{i}{h}") for h in range(2)] for i in range(2)]
        s_vps = sem("s_vps")
        s_v = sem("s_v")
        s_kps = sem("s_kps")
        s_krelu = sem("s_krelu")
        s_kact = sem("s_kact")
        s_rps = sem("s_rps")
        s_thr = sem("s_thr")
        s_yps = sem("s_yps")
        s_y2 = sem("s_y2")
        s_thy = sem("s_thy")
        s_thq = sem("s_thq")
        s_gate = sem("s_gate")
        s_sA = sem("s_sA")
        s_ttr = sem("s_ttr")
        s_mhi = sem("s_mhi")
        s_mp = sem("s_mp")
        s_mps = [sem(f"s_mps{h}") for h in range(2)]
        s_mT = [sem(f"s_mT{h}") for h in range(2)]
        s_mout = [sem(f"s_mout{h}") for h in range(2)]
        s_min = [[sem(f"s_min{i}{h}") for h in range(2)] for i in range(2)]
        s_sB = sem("s_sB")
        s_add = sem("s_add")
        s_exp = sem("s_exp")
        s_pv = sem("s_pv")
        s_osb = sem("s_osb")
        s_oTps = sem("s_oTps")
        s_rsum = sem("s_rsum")
        s_on = sem("s_on")
        s_onTps = sem("s_onTps")
        s_onT = sem("s_onT")
        s_attps = sem("s_attps")
        s_xb = sem("s_xb")
        s_x1 = sem("s_x1")
        s_st2 = sem("s_st2")
        s_mv2 = sem("s_mv2")
        s_ln2 = sem("s_ln2")
        s_xh2 = sem("s_xh2")
        s_x1b = sem("s_x1b")
        s_x2Tps = sem("s_x2Tps")
        s_xmT = sem("s_xmT")
        s_upps = sem("s_upps")
        s_h = sem("s_h")
        s_dnps = sem("s_dnps")
        s_s1 = sem("s_s1")
        s_s2 = sem("s_s2")
        s_xc = [sem(f"s_xc{i}") for i in range(2)]
        s_yo = sem("s_yo")
        s_out = [sem(f"s_out{i}") for i in range(2)]

        FREED = {"max1": (s_mT[1], 1, 1), "xT": (s_xT, 1, 1), "oT": (s_on, 1, 1), "qk": (s_qkhi, 1, 1),
                 "onT": (s_onT, 1, 1), "att": (s_x1, 1, 1), "v": (s_v, 1, 1), "max0": (s_mT[0], 1, 1),
                 "k": (s_krelu, 1, 1), "x2T": (s_xmT, 1, 1), "up0": (s_h, 2, 1),
                 "up1": None,
                 "down": (s_s1, 1, 2), "r": (s_thr, 1, 1), "y": (s_y2, 1, 1)}

        def bank_free(eng, name, s):
            at = [j[0] for j in JOBS].index(name)
            back = [(j, 0) for j in JOBS[:at][::-1]] + [(j, n) for n in range(1, 4) for j in JOBS[::-1]]
            for (other, bank, lag), steps in back:
                b = s.minus(lag + steps)
                if bank == JOBS[at][1] and b.live():
                    if FREED[other]:
                        done, per, which = FREED[other]
                        wait(eng, done, count(per, b, which))
                    return

        def col(c):
            return cst[:, c:c + 1]

        def spread(c):
            return cst[:, c:c + EMB].unsqueeze(1).to_broadcast([128, TT, EMB])

        block = ctx.enter_context(nc.Block())

        @block.sync
        def _(sp):
            xv = x.rearrange("b (t p) e -> b p t e", p=TILE)
            ov = out.rearrange("b (t p) e -> b p t e", p=TILE)
            sp.dma_start(xin[:, 0], xv[0]).then_inc(s_xin[0], 16)
            sp.dma_start(cst[:], consts).then_inc(s_cst, 16)
            sp.dma_start(relA[:], rel_qk).then_inc(s_rela, 16)
            sp.dma_start(relB[:], rel_kq).then_inc(s_relb, 16)

            def stack_half(b, h):
                p = b.slot(2)
                heads = slice(h * HALF, h * HALF + HALF)
                sp.wait_ge(s_pout, count(16, b, 16))
                hold(sp, s_passs)
                wait(sp, s_sB, count(12, b.minus(2), 6 * h + 6))
                if h == 0:
                    wait(sp, s_init, 1 if b.first < 2 and b.turn is None else 0)
                for block in range(BLOCKS):
                    n, row = BLOCKS - block, (3 * block - block * (block - 1) // 2) * HEAD_DIM
                    rows = slice(row, row + n * HEAD_DIM)
                    sp.dma_start(qst[rows, p, heads, :], parts_dram[p, 0, 0:n, :, heads, :].rearrange(
                        "c d h q -> (c d) (h q)")).then_inc(s_st[p][h], 16)
                    sp.dma_start(kst[rows, p, heads, :], parts_dram[p, 1, block:block + 1, :, heads, :].rearrange(
                        "c d h q -> c d (h q)").to_broadcast([n, HEAD_DIM, HALF * SEQ])).then_inc(s_st[p][h], 16)

            def step(s):
                n, f, a, b, c = stages(s)
                if n.live() and (n.first > 0 or n.turn is not None):
                    wait(sp, s_xn, count(1, n, -1))
                    hold(sp, s_passs)
                    sp.dma_start(xin[:, n.slot(2)], xv[n.index()]).then_inc(s_xin[n.slot(2)], 16)
                if c.live():
                    sp.dma_start(xc[:, c.slot(2)], xv[c.index()]).then_inc(s_xc[c.slot(2)], 16)
                if f.live():
                    p = f.slot(2)
                    sp.wait_ge(s_low, count(1, f, 1))
                    hold(sp, s_passs)
                    wait(sp, s_st[p][1], count2(STACK_DMAS, f, 0))
                    sp.dma_start(parts_dram[p].rearrange("i c d h q -> (d h) (i c) q"),
                                 parts[:, p].rearrange("p i c q -> p (i c) q")).then_inc(s_pout, 16)
                    stack_half(f, 0)
                if c.live():
                    sp.wait_ge(s_yo, count(1, c, 1))
                    hold(sp, s_passs)
                    sp.dma_start(ov[c.index()], yo[:, c.slot(2)]).then_inc(s_out[c.slot(2)], 16)
                if f.live():
                    stack_half(f, 1)
                if c.live():
                    sp.wait_ge(s_out[c.slot(2)], count2(16, c, 16))
                    hold(sp, s_passs)

            each_step(sp, step)
            for o in s_out:
                sp.wait_ge(o, 16 * BATCHES // 2)

        @block.gpsimd
        def _(pool):
            nc.gpsimd.memset(neghalf[:], -0.5).then_inc(s_initp, 1)
            nc.gpsimd.memset(xn0T[:, :, 0:1], 0.0).then_inc(s_initp, 1)

            def init_v():
                nc.gpsimd.memset(vst[:], 0.0).then_inc(s_initp, 1)
                pool.wait_ge(s_initp, 3)
                for gg in range(2):
                    ones = vst[:].rearrange("p s t (m g) w -> p (s t m) g w", g=2)[:, :, gg, 16 + 8 * gg:17 + 8 * gg]
                    nc.gpsimd.memset(ones, 1.0).then_inc(s_initp, 1)

            init_v()

            def step(s):
                n, f, a, b, c = stages(s)
                if c.live():
                    pool.wait_ge(s_cst, 16)
                    nc.gpsimd.tensor_tensor(xb[:], xn0[:, c.slot(4)], spread(C_BO), ALU.add).then_inc(s_xb, 1)
                if f.live():
                    p = f.slot(2)
                    pool.wait_ge(s_xT, count(1, f, 1))
                    wait(pool, s_xrk, count(1, f, 0))
                    nc.gpsimd.tensor_tensor(dx[:], xn0T[:, p, 1:SEQ + 1], xn0T[:, p, 0:SEQ],
                                            ALU.subtract).then_inc(s_dx, 1)
                    pool.wait_ge(s_qkhi, count(1, f, 1))
                    nc.gpsimd.tensor_tensor(rest[:], qk32[:], parts[:, p, :, 0], ALU.subtract).then_inc(s_rest, 1)
                    pool.wait_ge(s_mid, count(1, f, 1))
                    nc.gpsimd.tensor_tensor(parts[:, p, :, 2], rest[:], parts[:, p, :, 1],
                                            ALU.subtract).then_inc(s_low, 1)
                if f.live():
                    pool.wait_ge(s_krelu, count(1, f, 1))
                    wait(pool, s_yps, count(1, f, 0))
                    nc.gpsimd.tensor_tensor(kact[:], krelu[:], krelu[:], ALU.mult).then_inc(s_kact, 1)
                if c.live():
                    pool.wait_ge(s_mv2, count(1, c, 1))
                    hold(pool, s_passp)
                    nc.gpsimd.tensor_scalar(lnv2[:, 0], mv2[:, :, 0], -1.0, 1.0, ALU.mult,
                                            ALU.mult).then_inc(s_ln2, 1)
                    nc.gpsimd.tensor_scalar(lnv2[:, 1], mv2[:, :, 1], EPS, 1.0, ALU.add,
                                            ALU.mult).then_inc(s_ln2, 1)
                    pool.wait_ge(s_ln2, count(3, c, 2))
                    nc.gpsimd.tensor_tensor(lnv2[:, 2], lnv2[:, 1], neghalf[:], ALU.pow).then_inc(s_ln2, 1)
                    pool.wait_ge(s_ln2, count(3, c, 3))
                    hold(pool, s_passp)
                    for t in range(TT):
                        ins = nc.gpsimd.tensor_scalar(xh2[:, t], x1[:, t], lnv2[:, 0, t:t + 1],
                                                      lnv2[:, 2, t:t + 1], ALU.add, ALU.mult)
                    ins.then_inc(s_xh2, 1)
                    nc.gpsimd.tensor_tensor(x1b[:], x1[:], spread(C_B2), ALU.add).then_inc(s_x1b, 1)
                if n.live():
                    pool.wait_ge(s_mv, count(1, n, 1))
                    nm, a0, rs0, v1, v2, a1_, rs1 = [lnv[:, i] for i in range(7)]
                    v = mv[:, :, 1]
                    hold(pool, s_passp)
                    nc.gpsimd.tensor_scalar(nm, mv[:, :, 0], -1.0, 1.0, ALU.mult, ALU.mult).then_inc(s_ln, 1)
                    nc.gpsimd.tensor_scalar(a0, v, EPS, 1.0, ALU.add, ALU.mult).then_inc(s_ln, 1)
                    pool.wait_ge(s_ln, count(7, n, 2))
                    nc.gpsimd.tensor_tensor(rs0, a0, neghalf[:], ALU.pow).then_inc(s_ln, 1)
                    pool.wait_ge(s_ln, count(7, n, 3))
                    nc.gpsimd.tensor_tensor(v1, v, rs0, ALU.mult).then_inc(s_ln, 1)
                    pool.wait_ge(s_ln, count(7, n, 4))
                    nc.gpsimd.tensor_tensor(v2, v1, rs0, ALU.mult).then_inc(s_ln, 1)
                    pool.wait_ge(s_ln, count(7, n, 5))
                    hold(pool, s_passp)
                    nc.gpsimd.tensor_scalar(a1_, v2, EPS, 1.0, ALU.add, ALU.mult).then_inc(s_ln, 1)
                    pool.wait_ge(s_ln, count(7, n, 6))
                    nc.gpsimd.tensor_tensor(rs1, a1_, neghalf[:], ALU.pow).then_inc(s_ln, 1)
                    for t in range(TT):
                        ins = nc.gpsimd.tensor_scalar(xn0[:, n.slot(4), t], xin[:, n.slot(2), t], nm[:, t:t + 1],
                                                      rs0[:, t:t + 1], ALU.add, ALU.mult)
                        ins.then_inc(s_xa, 1)
                    pool.wait_ge(s_ln, count(7, n, 7))
                    pool.wait_ge(s_xa, count(2, n, 2))
                    hold(pool, s_passp)
                    for t in range(TT):
                        ins = nc.gpsimd.tensor_scalar(xh[:, n.slot(2), t], xn0[:, n.slot(4), t], rs1[:, t:t + 1],
                                                      1.0, ALU.mult, ALU.mult)
                    ins.then_inc(s_xn, 1)
                if f.live():
                    pool.wait_ge(s_thy, count(1, f, 1))
                    hold(pool, s_passp)
                    nc.gpsimd.tensor_scalar(thq[:], thy[:], 0.25, 0.25, ALU.mult, ALU.add).then_inc(s_thq, 1)
                    pool.wait_ge(s_thq, count(1, f, 1))
                    nc.gpsimd.tensor_tensor(gate[:, f.slot(4)], thq[:], y2[:], ALU.mult).then_inc(s_gate, 1)
                if c.live():
                    pool.wait_ge(s_s1, count(1, c, 2))
                    nc.gpsimd.tensor_tensor(s2[:], s1[:], gate[:, c.slot(4)], ALU.mult).then_inc(s_s2, 1)
                    pool.wait_ge(s_s2, count(1, c, 1))
                    pool.wait_ge(s_xc[c.slot(2)], count2(16, c, 16))
                    nc.gpsimd.tensor_tensor(yo[:, c.slot(2)], s2[:].rearrange("p (t e) -> p t e", t=TT),
                                            xc[:, c.slot(2)], ALU.add).then_inc(s_yo, 1)

            each_step(pool, step)

        @block.scalar
        def _(act):
            def exp_unit(b, u):
                if u in ADDED:
                    act.wait_ge(s_add, count(len(ADDED), b, ADDED.index(u) + 1))
                else:
                    act.wait_ge(s_sB, count(12, b, u + 1))
                wait(act, s_pv, count(4, b, u // 3 - 1))
                nc.scalar.activation(prob[:, u % 6], psB[u % 3][:], ACT.Exp).then_inc(s_exp, 1)

            def turned_max(b, h):
                bank = psP[BANK[f"max{h}"]]
                act.wait_ge(s_mps[h], count(1, b, 1))
                nc.scalar.activation(maxT[:, h, :], bank[0:2 * HALF * TT, 0:TILE // 2].bitcast(BF16),
                                     ACT.Copy).then_inc(s_mT[h], 1)
                act.wait_ge(s_mT[h], count(1, b, 1))
                act.dma_start(max_dram[b.slot(2), h].rearrange("c (n q) -> (c n) q", q=TILE),
                              maxT[:, h, :]).then_inc(s_mout[h], 16)

            def max_rows(b, h):
                p = b.slot(2)
                act.wait_ge(s_mout[h], count(16, b, 16))
                act.dma_start(qst[M_ROW:M_ROW + 2, p, h * HALF:(h + 1) * HALF, :],
                              max_dram[p, h].rearrange("c (h q) -> c h q", q=SEQ)).then_inc(s_min[p][h], 16)

            def step(s):
                n, f, a, b, c = stages(s)

                def units(*us):
                    for u in us:
                        if b.live():
                            exp_unit(b, u)

                if s.first == 0 and s.turn is None:
                    act.wait_ge(s_cst, 16)
                    act.wait_ge(s_initp, 2)
                    act.wait_ge(s_bqs, 1)
                if c.live():
                    exp_unit(c, UNITS - 1)
                if b.live():
                    turned_max(b, 1)
                if f.live():
                    p = f.slot(2)
                    ps = psP[BANK["xT"]]
                    act.wait_ge(s_xTps, count(1, f, 1))
                    wait(act, s_xrk, count(1, f, -1))
                    wait(act, s_dx, count(1, f, -1))
                    nc.scalar.activation(xn0T[:, p, 1:SEQ + 1], ps[:, 0:SEQ], ACT.Copy)
                    nc.scalar.activation(xn1T[:, p], ps[:, SEQ:2 * SEQ], ACT.Identity, scale=col(C_G1),
                                         bias=col(C_L1)).then_inc(s_xT, 1)
                units(0, 1)
                if c.live():
                    act.wait_ge(s_pv, count(4, c, 4))
                    nc.scalar.activation(osb[:], psO[:], ACT.Copy).then_inc(s_osb, 1)
                if f.live():
                    ps = psP[BANK["qk"]]
                    act.wait_ge(s_qkps, count(1, f, 1))
                    wait(act, s_rest, count(1, f, 0))
                    wait(act, s_pout, count(16, f.minus(1), 0))
                    for q_dst, k_dst in ((qk32[:, 0], qk32[:, 1]), (parts[:, p, 0, 0], parts[:, p, 1, 0])):
                        nc.scalar.activation(q_dst, ps[:, 0:SEQ], ACT.Identity, scale=QSCALE, bias=bqs[:])
                        ins = nc.scalar.activation(k_dst, ps[:, SEQ:2 * SEQ], ACT.Identity, bias=col(C_BK))
                    ins.then_inc(s_qkhi, 1)
                units(2)
                if f.live():
                    if f.first == 0 and f.turn is None:
                        act.wait_ge(s_initp, 5)
                    act.wait_ge(s_vps, count(1, f, 1))
                    dst = vst[:, f.slot(4)].rearrange("p t h w -> p (t h w)")
                    dst = bass.AP(dst.tensor, dst.offset,
                                  [list(dst.ap[0]), [64, TT * HEADS // 2], [32 + HEAD_DIM, 2], [1, HEAD_DIM]])
                    nc.scalar.activation(dst, psP[BANK["v"]][:, 0:SEQ].rearrange("p (m g w) -> p m g w", g=2, w=8),
                                         ACT.Copy).then_inc(s_v, 1)
                units(3)
                if b.live():
                    max_rows(b, 1)
                if f.live():
                    act.wait_ge(s_rest, count(1, f, 1))
                    nc.scalar.activation(parts[:, p, :, 1], rest[:], ACT.Copy).then_inc(s_mid, 1)
                units(4)
                if c.live():
                    act.wait_ge(s_onTps, count(1, c, 1))
                    nc.scalar.activation(onT[:], psP[BANK["onT"]][:, 0:SEQ], ACT.Identity,
                                         bias=col(C_BV)).then_inc(s_onT, 1)
                if f.live():
                    act.wait_ge(s_kps, count(1, f, 1))
                    wait(act, s_kact, count(1, f, 0))
                    nc.scalar.activation(krelu[:], psP[BANK["k"]][:, 0:SEQ], ACT.Relu).then_inc(s_krelu, 1)
                units(5)
                if a.live():
                    turned_max(a, 0)
                if f.live():
                    act.wait_ge(s_rps, count(1, f, 1))
                    wait(act, s_y2, count(1, f, 0))
                    nc.scalar.activation(thr[:], psP[BANK["r"]][:, 0:SEQ], ACT.Tanh, scale=0.5).then_inc(s_thr, 1)
                units(6, 7)
                if c.live():
                    act.wait_ge(s_x2Tps, count(1, c, 1))
                    nc.scalar.activation(xmT[:], psP[BANK["x2T"]][:, 0:SEQ], ACT.Identity, scale=col(C_G2),
                                         bias=col(C_L2)).then_inc(s_xmT, 1)
                units(8)
                if a.live():
                    max_rows(a, 0)

                def hidden(i):
                    if c.live():
                        act.wait_ge(s_upps, count(2, c, i + 1))
                        for j in range(2):
                            k = 2 * i + j
                            ins = nc.scalar.activation(hT[:, k], psP[BANK[f"up{i}"]][:, j * SEQ:(j + 1) * SEQ],
                                                       ACT.Relu, bias=col(C_B1 + k))
                        ins.then_inc(s_h, 1)

                hidden(0)
                units(9)
                hidden(1)
                units(10)
                if f.live():
                    act.wait_ge(s_y2, count(1, f, 1))
                    wait(act, s_thq, count(1, f, 0))
                    nc.scalar.activation(thy[:], y2[:], ACT.Tanh, scale=0.25).then_inc(s_thy, 1)

            each_step(act, step)

        @block.vector
        def _(dve):
            def init_stacks():
                nc.vector.memset(qst[:].bitcast(F32), 0.0).then_inc(s_initv, 1)
                nc.vector.memset(kst[:].bitcast(F32), 0.0).then_inc(s_initv, 1)
                dve.wait_ge(s_initv, 2)
                nc.vector.memset(kst[M_ROW:M_ROW + 2].bitcast(F32), 1 + 0x3F80 / 2 ** 23).then_inc(s_init, 1)
                nc.vector.tensor_copy(identb[:], ident).then_inc(s_init, 1)
                nc.vector.tensor_copy(identr[:], ident).then_inc(s_init, 1)

            def init_rel():
                dve.wait_ge(s_relb, 16)
                nc.vector.tensor_copy(relBh[:], relB[:]).then_inc(s_relh, 1)
                dve.wait_ge(s_relh, 1)
                nc.vector.tensor_tensor(relBl[:], relB[:], relBh[:].bitcast(F32), ALU.subtract).then_inc(s_relh, 1)

            def ttr(b, h):
                bank = psA[h % 2]
                dve.wait_ge(s_sA, count(16, b, h + 1))
                hold(dve, s_passd)
                for t in range(TT):
                    s = bank[:, 0:TILE] if t == 0 else bank[:, TILE:TILE + SEQ]
                    ins = nc.vector.tensor_tensor_reduce(
                        out=s, in0=s, in1=relA[:, h, SEQ - (t + 1) * TILE:SEQ], scale=1.0, scalar=MASKED,
                        op0=ALU.add, op1=ALU.max, accum_out=mx[:, h, t:t + 1])
                ins.then_inc(s_ttr, 1)

            def add_rel(b, u):
                heads, width = unit_heads(u)
                bank = psB[u % 3][:].rearrange("p (n q) -> p n q", q=width)
                dve.wait_ge(s_sB, count(12, b, u + 1))
                nc.vector.tensor_tensor(bank, bank, relB[:, heads[0]:heads[-1] + 1:2, 0:width],
                                        ALU.add).then_inc(s_add, 1)

            def max_parts(b, h):
                m = mx[:, h * HALF:(h + 1) * HALF, :].rearrange("p h t -> p (h t)")
                dve.wait_ge(s_ttr, count(16, b, (h + 1) * HALF))
                wait(dve, s_mps[h], count(1, b, 0))
                nc.vector.tensor_scalar(mparts[:, h, 0], m, -1.0, None, ALU.mult).then_inc(s_mhi, 1)
                dve.wait_ge(s_mhi, count(2, b, h + 1))
                nc.vector.scalar_tensor_tensor(out=mparts[:, h, 1], in0=m, scalar=-1.0, in1=mparts[:, h, 0],
                                               op0=ALU.mult, op1=ALU.subtract).then_inc(s_mp, 1)

            def layer_stats(src, st, mvt, s_own, s_done, own_value):
                for t in range(TT):
                    ins = nc.vector.bn_stats(st[:, t], src[:, t])
                ins.then_inc(s_own, 1)
                dve.wait_ge(s_own, own_value)
                hold(dve, s_passd)
                for t in range(TT):
                    ins = nc.vector.bn_aggr(mvt[:, t], st[:, t])
                ins.then_inc(s_done, 1)

            def step(s):
                n, f, a, b, c = stages(s)
                if s.first == -1 and s.turn is None:
                    nc.vector.memset(s1[:], 0.0).then_inc(s_s1, 1)
                if s.first == 1 and s.turn is None:
                    dve.wait_ge(s_rela, 16)

                def heads(*hs):
                    for h in hs:
                        if a.live():
                            ttr(a, h)
                        if b.live() and UNIT_AT.get(h - 1) in ADDED:
                            add_rel(b, UNIT_AT[h - 1])

                heads(0, 1, 2, 3)
                if f.live():
                    p = f.slot(2)
                    dve.wait_ge(s_dx, count(1, f, 1))
                    wait(dve, s_rps, count(1, f, 0))
                    prev = xn0T[:, p, 0:SEQ]
                    nc.vector.scalar_tensor_tensor(out=xkT[:], in0=dx[:], scalar=col(C_MK), in1=prev,
                                                   op0=ALU.mult, op1=ALU.add)
                    nc.vector.scalar_tensor_tensor(out=xrT[:], in0=dx[:], scalar=col(C_MR), in1=prev,
                                                   op0=ALU.mult, op1=ALU.add).then_inc(s_xrk, 1)
                heads(4, 5)
                if c.live():
                    o = psP[BANK["oT"]][:].rearrange("p (m w) -> p m w", w=32)
                    sums = o[:, :, 16:32].rearrange("p m (g w) -> p m g w", g=2)[:, :, :, 0]
                    outs = o[:, :, 0:16].rearrange("p m (g w) -> p m g w", g=2)
                    dve.wait_ge(s_oTps, count(1, c, 1))
                    nc.vector.reciprocal(rsum[:].rearrange("p (m g) -> p m g", g=2), sums).then_inc(s_rsum, 1)
                    dve.wait_ge(s_rsum, count(1, c, 1))
                    nc.vector.tensor_tensor(
                        on[:].rearrange("p (m g w) -> p m g w", g=2, w=8), outs,
                        rsum[:].rearrange("p (m g) -> p m g", g=2).unsqueeze(3).to_broadcast([128, 16, 2, 8]),
                        ALU.mult).then_inc(s_on, 1)
                heads(6, 7)
                if a.live():
                    max_parts(a, 0)
                heads(8)
                if c.live():
                    dve.wait_ge(s_attps, count(1, c, 1))
                    dve.wait_ge(s_xb, count(1, c, 1))
                    nc.vector.tensor_tensor(x1[:], psP[BANK["att"]][:, 0:SEQ].rearrange("p (t e) -> p t e", t=TT),
                                            xb[:], ALU.add).then_inc(s_x1, 1)
                    dve.wait_ge(s_x1, count(1, c, 1))
                    layer_stats(x1, stats2, mv2, s_st2, s_mv2, count(1, c, 1))
                heads(9, 10, 11)
                if f.live():
                    dve.wait_ge(s_yps, count(1, f, 1))
                    dve.wait_ge(s_thr, count(1, f, 1))
                    wait(dve, s_gate, count(1, f, 0))
                    nc.vector.scalar_tensor_tensor(out=y2[:], in0=thr[:], scalar=1.0, in1=psP[BANK["y"]][:, 0:SEQ],
                                                   op0=ALU.add, op1=ALU.mult).then_inc(s_y2, 1)
                if n.live():
                    dve.wait_ge(s_xin[n.slot(2)], count2(16, n, 16))
                    wait(dve, s_ln, count(7, n, 0))
                    layer_stats(xin[:, n.slot(2)], stats, mv, s_stats, s_mv, count(1, n, 1))
                if s.first == -1 and s.turn is None:
                    dve.wait_ge(s_cst, 16)
                    nc.vector.tensor_scalar(bqs[:], col(C_BQ), QSCALE, None, ALU.mult).then_inc(s_bqs, 1)
                    init_stacks()
                if s.first == 0 and s.turn is None:
                    init_rel()
                heads(12, 13, 14, 15)
                if a.live():
                    max_parts(a, 1)
                if c.live():
                    dve.wait_ge(s_dnps, count(1, c, 1))
                    dve.wait_ge(s_x1b, count(1, c, 1))
                    nc.vector.tensor_tensor(s1[:], psP[BANK["down"]][:, 0:SEQ], x1b[:].rearrange("p t e -> p (t e)"),
                                            ALU.add).then_inc(s_s1, 1)

            each_step(dve, step)

        @block.tensor
        def _(pe):
            def a_unit(b, h):
                p, bank = b.slot(2), psA[h % 2]
                if h % HALF == 0:
                    pe.wait_ge(s_st[p][h // HALF], count2(STACK_DMAS, b, STACK_DMAS))
                wait(pe, s_ttr, count(16, b, h - 1))
                nc.tensor.matmul(bank[:, 0:TILE], qst[0:A_ROWS, p, h, 0:TILE], kst[0:A_ROWS, p, h, 0:TILE],
                                 start=True, stop=True)
                nc.tensor.matmul(bank[:, TILE:TILE + SEQ], qst[0:A_ROWS, p, h, TILE:SEQ], kst[0:A_ROWS, p, h, :],
                                 start=True, stop=True).then_inc(s_sA, 1)

            def b_unit(b, u):
                p, grp, i = b.slot(2), u // 3, u % 3
                bank = psB[i]
                if u % 6 == 0:
                    pe.wait_ge(s_min[p][u // 6], count2(16, b, 16))
                wait(pe, s_exp, count(12, b, u - 2))
                heads, width = unit_heads(u)
                for n, rel in enumerate((relBh, relBl) if u not in ADDED else ()):
                    nc.tensor.matmul(bank[:], identr[:], rel[:, heads[0]:heads[-1] + 1:2, 0:width],
                                     start=(n == 0), stop=False, skip_group_check=True)
                keys = slice(0, TILE) if i < 2 else slice(TILE, SEQ)
                for j, h in enumerate(heads):
                    ins = nc.tensor.matmul(bank[:, j * width:(j + 1) * width], kst[0:B_ROWS, p, h, keys],
                                           qst[0:B_ROWS, p, h, SEQ - width:SEQ],
                                           start=(j == 0 and u in ADDED),
                                           stop=(j == len(heads) - 1), skip_group_check=True)
                ins.then_inc(s_sB, 1)

            def pv(b, grp):
                if grp == 0:
                    pe.wait_ge(s_v, count(1, b, 1))
                    wait(pe, s_osb, count(1, b, 0))
                pe.wait_ge(s_exp, count(12, b, 3 * grp + 3))
                u, gg = grp // 2, grp % 2
                for kt in range(TT):
                    for j in range(GROUP):
                        w = vst[:, b.slot(4), kt, group_heads(grp)[j], :]
                        if kt == 0:
                            o = psO[32 * j:32 * j + 32, u * SEQ:(u + 1) * SEQ]
                            pr = prob[:, 3 * gg + j // 2, (j % 2) * SEQ:(j % 2 + 1) * SEQ]
                        else:
                            o = psO[32 * j:32 * j + 32, u * SEQ + TILE:(u + 1) * SEQ]
                            pr = prob[:, 3 * gg + 2, j * TILE:(j + 1) * TILE]
                        ins = nc.tensor.matmul(o, w, pr, start=(gg == 0 and kt == 0), stop=(gg == 1 and kt == 1),
                                               skip_group_check=True)
                ins.then_inc(s_pv, 1)

            def turned_max(b, h):
                bank = psP[BANK[f"max{h}"]]
                pe.wait_ge(s_mp, count(2, b, h + 1))
                nc.tensor.transpose(bank[0:2 * HALF * TT, 0:TILE // 2].bitcast(BF16),
                                    mparts[:, h].rearrange("p c n -> p (c n)"), identb[:]).then_inc(s_mps[h], 1)

            def turn(dst, src):
                return nc.tensor.transpose(dst, src, ident)

            def job(name, s, b):
                if not b.live():
                    return
                bank_free(pe, name, s)
                ps = psP[BANK[name]]
                p = b.slot(2)
                if name == "max1":
                    turned_max(b, 1)
                elif name == "max0":
                    turned_max(b, 0)
                elif name == "xT":
                    pe.wait_ge(s_xn, count(1, b, 1))
                    for t in range(TT):
                        turn(ps[:, t * TILE:(t + 1) * TILE], xn0[:, b.slot(4), t])
                    for t in range(TT):
                        ins = turn(ps[:, SEQ + t * TILE:SEQ + (t + 1) * TILE], xh[:, p, t])
                    ins.then_inc(s_xTps, 1)
                elif name == "qk":
                    pe.wait_ge(s_xT, count(1, b, 1))
                    for i in range(2):
                        ins = nc.tensor.matmul(ps[:, i * SEQ:(i + 1) * SEQ],
                                               cst[:, C_WQKV + i * EMB:C_WQKV + (i + 1) * EMB], xn1T[:, p],
                                               start=True, stop=True)
                    ins.then_inc(s_qkps, 1)
                elif name == "v":
                    for t in range(TT):
                        ins = nc.tensor.matmul(ps[:, t * EMB:(t + 1) * EMB], xn1T[:, p, t * TILE:(t + 1) * TILE],
                                               cst[:, C_WQKV + 2 * EMB:C_WQKV + 3 * EMB], start=True, stop=True)
                    ins.then_inc(s_vps, 1)
                elif name == "k":
                    pe.wait_ge(s_xrk, count(1, b, 1))
                    nc.tensor.matmul(ps[:, 0:SEQ], cst[:, C_WK:C_WK + EMB], xkT[:], start=True,
                                     stop=True).then_inc(s_kps, 1)
                elif name == "r":
                    for t in range(TT):
                        ins = nc.tensor.matmul(ps[:, t * EMB:(t + 1) * EMB], xrT[:, t * TILE:(t + 1) * TILE],
                                               cst[:, C_WR:C_WR + EMB], start=True, stop=True)
                    ins.then_inc(s_rps, 1)
                elif name == "y":
                    pe.wait_ge(s_kact, count(1, b, 1))
                    for t in range(TT):
                        ins = nc.tensor.matmul(ps[:, t * EMB:(t + 1) * EMB], kact[:, t * TILE:(t + 1) * TILE],
                                               cst[:, C_WV:C_WV + EMB], start=True, stop=True)
                    ins.then_inc(s_yps, 1)
                elif name == "oT":
                    pe.wait_ge(s_osb, count(1, b, 1))
                    for t in range(TT):
                        for u in range(2):
                            ins = turn(ps[:, (2 * t + u) * TILE:(2 * t + u + 1) * TILE],
                                       osb[:, u * SEQ + t * TILE:u * SEQ + (t + 1) * TILE])
                    ins.then_inc(s_oTps, 1)
                elif name == "onT":
                    pe.wait_ge(s_on, count(1, b, 1))
                    for t in range(TT):
                        ins = turn(ps[:, t * TILE:(t + 1) * TILE], on[:, t * EMB:(t + 1) * EMB])
                    ins.then_inc(s_onTps, 1)
                elif name == "att":
                    pe.wait_ge(s_onT, count(1, b, 1))
                    for t in range(TT):
                        ins = nc.tensor.matmul(ps[:, t * EMB:(t + 1) * EMB], onT[:, t * TILE:(t + 1) * TILE],
                                               cst[:, C_WO:C_WO + EMB], start=True, stop=True)
                    ins.then_inc(s_attps, 1)
                elif name == "x2T":
                    pe.wait_ge(s_xh2, count(1, b, 1))
                    for t in range(TT):
                        ins = turn(ps[:, t * TILE:(t + 1) * TILE], xh2[:, t])
                    ins.then_inc(s_x2Tps, 1)
                elif name in ("up0", "up1"):
                    i = int(name[-1])
                    pe.wait_ge(s_xmT, count(1, b, 1))
                    for j in range(2):
                        k = 2 * i + j
                        ins = nc.tensor.matmul(ps[:, j * SEQ:(j + 1) * SEQ],
                                               cst[:, C_W1 + k * TILE:C_W1 + (k + 1) * TILE], xmT[:],
                                               start=True, stop=True)
                    ins.then_inc(s_upps, 1)
                elif name == "down":
                    pe.wait_ge(s_h, count(2, b, 2))
                    for t in range(TT):
                        for k in range(FT):
                            ins = nc.tensor.matmul(ps[:, t * EMB:(t + 1) * EMB], hT[:, k, t * TILE:(t + 1) * TILE],
                                                   cst[:, C_W2 + k * EMB:C_W2 + (k + 1) * EMB],
                                                   start=(k == 0), stop=(k == FT - 1))
                    ins.then_inc(s_dnps, 1)

            AT = {1: ["max1", "xT"], 3: ["qk"], 5: ["oT", "v"], 7: ["onT", "k"], 8: ["att"],
                  9: ["max0", "r"], 10: ["y"], 12: ["x2T"], 13: ["up0"], 14: ["up1"], 15: ["down"]}
            LAGS = {name: lag for name, _, lag in JOBS}

            def step(s):
                n, f, a, b, c = stages(s)
                if s.first == 0 and s.turn is None:
                    pe.wait_ge(s_cst, 16)
                if s.first == 1 and s.turn is None:
                    pe.wait_ge(s_init, 3)
                if s.first == 2 and s.turn is None:
                    pe.wait_ge(s_relh, 2)
                for i in range(HEADS):
                    if a.live():
                        a_unit(a, i)
                    if i % 4 == 3:
                        if i == 3:
                            if c.live():
                                pv(c, GROUPS - 1)
                        elif b.live():
                            pv(b, i // 4 - 1)
                    elif b.live():
                        b_unit(b, UNIT_AT[i])
                    for name in AT.get(i, []):
                        job(name, s, s.minus(LAGS[name]))

            each_step(pe, step)


_OUT = (BATCHES, SEQ, EMB)


def kernel(**inputs):
    import concourse.bacc as _bacc
    from concourse.bass_utils import run_bass_kernel_spmd as _run

    a = {k: np.asarray(v) for k, v in inputs.items()}

    def t(w):
        return np.ascontiguousarray(w.T)

    def row(v):
        return np.tile(v[None, :], (128, 1))

    w2 = t(a["L0_attn_w2"]).reshape(FT, TILE, EMB).transpose(1, 0, 2).reshape(TILE, HIDDEN)
    order = np.arange(EMB).reshape(HEADS, HEAD_DIM).T.reshape(-1)
    w3 = a["L0_attn_in_proj_w"].reshape(3, EMB, EMB)
    wqkv = np.concatenate([t(w3[0][order]), t(w3[1][order]), t(w3[2])], axis=1)
    bqkv = a["L0_attn_in_proj_b"].reshape(3, EMB)
    consts = np.concatenate([
        wqkv, t(a["L0_attn_out_w"]), t(a["L0_attn_w1"]), w2, t(a["L0_ffn_W_r"]), t(a["L0_ffn_W_k"]),
        t(a["L0_ffn_W_v"]), np.eye(128, dtype=np.float32), row(a["L0_attn_out_b"]),
        row(a["L0_attn_b2"]), bqkv[0][order][:, None], bqkv[1][order][:, None], t(a["L0_attn_b1"].reshape(FT, TILE)),
        a["L0_attn_ln1_g"][:, None], a["L0_attn_ln1_b"][:, None], a["L0_attn_ln2_g"][:, None],
        a["L0_attn_ln2_b"][:, None], a["L0_ffn_mu_r"][:, None], a["L0_ffn_mu_k"][:, None], bqkv[2][:, None]], axis=1)
    rel = np.concatenate([np.full((HEADS, TILE), MASKED, np.float32), a["L0_attn_rel_pos"][:, :SEQ]], axis=1)
    i, j = np.arange(TILE)[:, None], np.arange(SEQ)[None, :]
    rel_kq = rel[:, TILE + j - i].transpose(1, 0, 2)
    rel_qk = rel[:, TILE + (SEQ - TILE) + i - j].transpose(1, 0, 2)

    nc = _bacc.Bacc("TRN2", target_bir_lowering=False, num_devices=1)
    arrays, args = {}, []
    for name, v in (("x", a["L0_attn_x"]), ("consts", consts), ("rel_kq", rel_kq), ("rel_qk", rel_qk)):
        arrays[f"in_{name}"] = np.ascontiguousarray(v)
        args.append(nc.dram_tensor(f"in_{name}", v.shape, F32, kind="ExternalInput").ap())
    args.append(nc.dram_tensor("out_0", _OUT, F32, kind="ExternalOutput").ap())
    gated_block(nc, *args)
    r = _run(nc, [arrays], core_ids=[0])
    return r.results[0]["out_0"]
```
